# Optimizing a Trainium2 kernel written in Bass

```python
import numpy as np
import jax
import jax.numpy as jnp

def _softmax(x, axis=-1):
    return jax.nn.softmax(x, axis=axis)

def _gelu(x):
    return jax.nn.gelu(x, approximate=True)

def _silu(x):
    return jax.nn.silu(x)

def _sigmoid(x):
    return jax.nn.sigmoid(x)

def _layernorm(x, axis=-1, eps=1e-05):
    m = jnp.mean(x, axis=axis, keepdims=True)
    v = jnp.var(x, axis=axis, keepdims=True)
    return (x - m) / jnp.sqrt(v + eps)

def _scatter_add(tgt, idx, src, axis=0):
    return tgt.at[idx].add(src)

def _segment_sum(src, seg, n):
    return jax.ops.segment_sum(src, seg, n)
kernel_name = 'mk_hybrid_d1_jaxref_r8_004daf'

def setup_inputs(seed: int=0):
    np.random.seed(seed)
    _w = jnp.asarray

    def _L0_attn_a_setup():
        import jax, jax.numpy as jnp
        import numpy as np
        B, N, E, H = (1, 512, 256, 16)
        D = E // H
        DEGREE = 4
        LN_EPS = 1e-05
        ROPE_BASE = 10000.0

        def rope_cos_sin(n, d):
            inv_freq = 1.0 / ROPE_BASE ** (jnp.arange(0, d, 2, dtype=jnp.float32) / d)
            t = jnp.arange(n, dtype=jnp.float32)[:, None] * inv_freq[None, :]
            return (jnp.cos(t), jnp.sin(t))

        def apply_rope(x, cos, sin):
            x1, x2 = jnp.split(x, 2, axis=-1)
            c = cos[None, :, None, :]
            s = sin[None, :, None, :]
            return jnp.concatenate([x1 * c - x2 * s, x1 * s + x2 * c], axis=-1)

        def layernorm(x, scale, bias, eps=LN_EPS):
            m = jnp.mean(x, axis=-1, keepdims=True)
            v = jnp.var(x, axis=-1, keepdims=True)
            return (x - m) * jax.lax.rsqrt(v + eps) * scale + bias

        def polynomial_attention(q, k, v, degree, is_causal):
            a = jnp.einsum('bhnd,bhmd->bhnm', q, k) ** degree
            if is_causal:
                a = jnp.tril(a)
            denom = jnp.sum(a, axis=-1, keepdims=True)
            return jnp.einsum('bhnm,bhmd->bhnd', a / denom, v)
        key = jax.random.key(seed)
        k0, k1, k2 = jax.random.split(key, 3)
        x = jax.random.normal(k0, (B, N, E), dtype=jnp.float32)
        w_qkv = jax.random.normal(k1, (E, 3 * E), dtype=jnp.float32) * (1.0 / np.sqrt(E))
        w_out = jax.random.normal(k2, (E, E), dtype=jnp.float32) * (1.0 / np.sqrt(E))
        ln_scale = jnp.ones((D,), dtype=jnp.float32)
        ln_bias = jnp.zeros((D,), dtype=jnp.float32)
        return {'x': x, 'w_qkv': w_qkv, 'w_out': w_out, 'ln_scale': ln_scale, 'ln_bias': ln_bias}
    _L0_attn_a_in = _L0_attn_a_setup()

    def _L0_attn_b_setup():
        import jax, jax.numpy as jnp
        import numpy as np
        NDIM = 16
        key = jax.random.key(seed)
        ks = jax.random.split(key, 5)
        L, B, D, N = (512, 8, 256, NDIM)
        return {'x': jax.random.normal(ks[0], (L, B, D), dtype=jnp.float32), 'delta': jax.random.normal(ks[1], (D, N, 1), dtype=jnp.float32), 'alpha': jax.random.normal(ks[2], (D, N, 1), dtype=jnp.float32), 'beta': jax.random.normal(ks[3], (D, N, 1), dtype=jnp.float32), 'gamma': jax.random.normal(ks[4], (D, N), dtype=jnp.float32)}
    _L0_attn_b_in = _L0_attn_b_setup()

    def _L0_ffn_setup():
        import jax, jax.numpy as jnp
        import numpy as np
        H, I, E, TOP_K = (256, 176, 16, 6)
        IS = 352
        NORM_TOPK_PROB = False

        def _silu_and_mul(gate_up):
            d = gate_up.shape[-1] // 2
            g, u = (gate_up[..., :d], gate_up[..., d:])
            return jax.nn.silu(g) * u
        key = jax.random.key(seed)
        ks = jax.random.split(key, 6)
        s = 0.02
        return {'x': jax.random.normal(ks[0], (1, 256, H), jnp.float32), 'gate_w': jax.random.normal(ks[1], (E, H), jnp.float32) * s, 'w1': jax.random.normal(ks[2], (E, 2 * I, H), jnp.float32) * s, 'w2': jax.random.normal(ks[3], (E, H, I), jnp.float32) * s, 'shared_w1': jax.random.normal(ks[4], (2 * IS, H), jnp.float32) * s, 'shared_w2': jax.random.normal(ks[5], (H, IS), jnp.float32) * s}
    _L0_ffn_in = _L0_ffn_setup()
    _d = {'L0_attn_a_x': _L0_attn_a_in['x'], 'L0_attn_a_w_qkv': _L0_attn_a_in['w_qkv'], 'L0_attn_a_w_out': _L0_attn_a_in['w_out'], 'L0_attn_a_ln_scale': _L0_attn_a_in['ln_scale'], 'L0_attn_a_ln_bias': _L0_attn_a_in['ln_bias'], 'L0_attn_b_delta': _L0_attn_b_in['delta'], 'L0_attn_b_alpha': _L0_attn_b_in['alpha'], 'L0_attn_b_beta': _L0_attn_b_in['beta'], 'L0_attn_b_gamma': _L0_attn_b_in['gamma'], 'L0_ffn_gate_w': _L0_ffn_in['gate_w'], 'L0_ffn_w1': _L0_ffn_in['w1'], 'L0_ffn_w2': _L0_ffn_in['w2'], 'L0_ffn_shared_w1': _L0_ffn_in['shared_w1'], 'L0_ffn_shared_w2': _L0_ffn_in['shared_w2']}
    _x0 = _d['L0_attn_a_x']
    _d['L0_attn_a_x'] = jax.random.normal(jax.random.fold_in(jax.random.key(seed), 1), (4, 1024, 256), dtype=_x0.dtype)
    del _x0
    return _d

def reference(L0_attn_a_x, L0_attn_a_w_qkv, L0_attn_a_w_out, L0_attn_a_ln_scale, L0_attn_a_ln_bias, L0_attn_b_delta, L0_attn_b_alpha, L0_attn_b_beta, L0_attn_b_gamma, L0_ffn_gate_w, L0_ffn_w1, L0_ffn_w2, L0_ffn_shared_w1, L0_ffn_shared_w2):

    def _L0_attn_a_ref(x, w_qkv, w_out, ln_scale, ln_bias):
        import jax, jax.numpy as jnp
        import numpy as np
        B, N, E, H = (1, 512, 256, 16)
        D = E // H
        DEGREE = 4
        LN_EPS = 1e-05
        ROPE_BASE = 10000.0

        def rope_cos_sin(n, d):
            inv_freq = 1.0 / ROPE_BASE ** (jnp.arange(0, d, 2, dtype=jnp.float32) / d)
            t = jnp.arange(n, dtype=jnp.float32)[:, None] * inv_freq[None, :]
            return (jnp.cos(t), jnp.sin(t))

        def apply_rope(x, cos, sin):
            x1, x2 = jnp.split(x, 2, axis=-1)
            c = cos[None, :, None, :]
            s = sin[None, :, None, :]
            return jnp.concatenate([x1 * c - x2 * s, x1 * s + x2 * c], axis=-1)

        def layernorm(x, scale, bias, eps=LN_EPS):
            m = jnp.mean(x, axis=-1, keepdims=True)
            v = jnp.var(x, axis=-1, keepdims=True)
            return (x - m) * jax.lax.rsqrt(v + eps) * scale + bias

        def polynomial_attention(q, k, v, degree, is_causal):
            a = jnp.einsum('bhnd,bhmd->bhnm', q, k) ** degree
            if is_causal:
                a = jnp.tril(a)
            denom = jnp.sum(a, axis=-1, keepdims=True)
            return jnp.einsum('bhnm,bhmd->bhnd', a / denom, v)
        b, n, e = x.shape
        proj = x @ w_qkv
        q, k, v = jnp.split(proj, 3, axis=-1)
        q = q.reshape(b, n, H, D)
        k = k.reshape(b, n, H, D)
        v = v.reshape(b, n, H, D)
        cos, sin = rope_cos_sin(n, D)
        q = apply_rope(q, cos, sin)
        k = apply_rope(k, cos, sin)
        q = q.transpose(0, 2, 1, 3)
        k = k.transpose(0, 2, 1, 3)
        v = v.transpose(0, 2, 1, 3)
        q = layernorm(q, ln_scale, ln_bias)
        k = layernorm(k, ln_scale, ln_bias)
        out = polynomial_attention(q, k, v, DEGREE, True)
        out = out.transpose(0, 2, 1, 3).reshape(b, n, e)
        out = out @ w_out
        return out

    def _L0_attn_b_ref(x, delta, alpha, beta, gamma):
        import jax, jax.numpy as jnp
        import numpy as np
        NDIM = 16
        L, B, D = x.shape
        scale = jnp.sqrt(jnp.asarray(1.0 / NDIM, dtype=x.dtype))
        p = jax.nn.sigmoid(delta) * jax.nn.sigmoid(alpha)
        q = 1.0 - p
        g = gamma * scale
        xt = jnp.transpose(x, (1, 2, 0))
        log_q = jnp.log(q)
        vander = jnp.exp(jnp.arange(L, dtype=x.dtype)[None, None, :] * log_q)
        k = jnp.einsum('dnl,dn->dl', p * beta * vander, g)
        fft_len = 2 * L
        k_f = jnp.fft.rfft(k.astype(jnp.float32), n=fft_len)
        x_f = jnp.fft.rfft(xt.astype(jnp.float32), n=fft_len)
        out = jnp.fft.irfft(x_f * k_f, n=fft_len)[..., :L].astype(x.dtype)
        return jax.nn.silu(jnp.transpose(out, (2, 0, 1)))

    def _L0_ffn_ref(x, gate_w, w1, w2, shared_w1, shared_w2):
        import jax, jax.numpy as jnp
        import numpy as np
        H, I, E, TOP_K = (256, 176, 16, 6)
        IS = 352
        NORM_TOPK_PROB = False

        def _silu_and_mul(gate_up):
            d = gate_up.shape[-1] // 2
            g, u = (gate_up[..., :d], gate_up[..., d:])
            return jax.nn.silu(g) * u
        B, S, Hd = x.shape
        xf = x.reshape(-1, Hd)
        T = xf.shape[0]
        shared_out = _silu_and_mul(xf @ shared_w1.T) @ shared_w2.T
        logits = xf @ gate_w.T
        probs = jax.nn.softmax(logits.astype(jnp.float32), axis=-1)
        routing_weights, selected = jax.lax.top_k(probs, TOP_K)
        if NORM_TOPK_PROB:
            routing_weights = routing_weights / routing_weights.sum(-1, keepdims=True)
        combine = jnp.zeros((T, E), jnp.float32).at[jnp.arange(T)[:, None], selected].add(routing_weights).astype(x.dtype)
        gate_up = jnp.einsum('th,eoh->teo', xf, w1)
        act = _silu_and_mul(gate_up)
        moe_out = jnp.einsum('te,tei,ehi->th', combine, act, w2)
        return (moe_out + shared_out).reshape(B, S, Hd)
    x = L0_attn_a_x
    x = x + _L0_attn_a_ref(_layernorm(x, axis=-1), L0_attn_a_w_qkv, L0_attn_a_w_out, L0_attn_a_ln_scale, L0_attn_a_ln_bias)
    x = x + _L0_ffn_ref(_layernorm(x, axis=-1), L0_ffn_gate_w, L0_ffn_w1, L0_ffn_w2, L0_ffn_shared_w1, L0_ffn_shared_w2)
    x = x + _L0_attn_b_ref(_layernorm(x, axis=-1), L0_attn_b_delta, L0_attn_b_alpha, L0_attn_b_beta, L0_attn_b_gamma)
    x = x + _L0_ffn_ref(_layernorm(x, axis=-1), L0_ffn_gate_w, L0_ffn_w1, L0_ffn_w2, L0_ffn_shared_w1, L0_ffn_shared_w2)
    return x

_drawn_inputs = setup_inputs


def setup_inputs(seed=0):
    import zlib

    import numpy as np

    out = dict(_drawn_inputs(seed))
    spreads = {'L0_attn_a_ln_scale': (1.0, 0.2), 'L0_attn_a_ln_bias': (0.0, 0.1)}
    factors = {}
    for name, (base, spread) in spreads.items():
        noise = np.random.default_rng([zlib.crc32(name.encode()), seed]).standard_normal(out[name].shape)
        drawn = base * np.exp(spread * noise) if base else spread * noise
        out[name] = jnp.asarray(drawn.astype(out[name].dtype))
    for name, factor in factors.items():
        out[name] = (out[name] * factor).astype(out[name].dtype)
    return out
```

```python
from contextlib import ExitStack

import numpy as np

import concourse.bass as bass
from concourse import mybir

F32 = mybir.dt.float32
F32R = mybir.dt.float32r
BF16 = mybir.dt.bfloat16
ACT = mybir.ActivationFunctionType
ALU = mybir.AluOpType
AX = mybir.AxisListType

P = 128
B, N, E = 4, 1024, 256
H, D = 16, 16
KE = E // P
NT = N // P
G = 4
NG = NT // G
GT = G * P
H2 = 2 * H
PARTS = 6
KP = PARTS * D
EPS = 1e-5
ONE = 1

NX, TOPK, IH, SH = 16, 6, 176, 352
FM = NX * IH // P
FC = FM + -(-SH // P)
VW = 32
Q = 4
RA = 11
LAG = 8
LAGS = 4


def attention(nc, x, w_qkv, w_out, ln_affine, rope, ident_in, x1):
    ctx = ExitStack()
    with ctx:
        def sb(name, shape, dt=F32):
            return ctx.enter_context(nc.sbuf_tensor(name, shape, dt))

        def sem(name):
            return ctx.enter_context(nc.semaphore(name))

        psum = ctx.enter_context(nc.psum_tensor("attn_psum", [P, 8, 512], F32))

        ident = sb("a_ident", [P, P])
        ident_bf = sb("a_ident_bf", [P, P], BF16)
        rope_sb = sb("rope_sb", [P, 2, NT, D])
        affine = sb("affine", [P, 2, D])
        neg_half = sb("neg_half", [P, G])
        wq_h = sb("wq_h", [P, KE, 3 * E], F32R)
        wq_l = sb("wq_l", [P, KE, 3 * E], F32R)
        wo = sb("wo_sb", [P, KE, E])
        xa = sb("xa", [P, NT, E])
        xr = sb("xr", [P, NT, E])
        stats = sb("stats", [P, NT, 6])
        mv = sb("mv", [P, NT, 2])
        rstd = sb("rstd", [P, NT])
        pad = sb("pad", [P, 1])
        eps = sb("eps", [P, G])
        head_eps = sb("head_eps", [P, 1])
        xn = sb("xn", [P, NG, G, E])
        xh = sb("xh", [P, NG, KE, GT], F32R)
        xl = sb("xl", [P, NG, KE, GT], F32R)
        mean = sb("hmean", [P, 8, H2])
        var = sb("hvar", [P, 8, H2])
        hr = sb("hr", [P, 8, H2])
        parts = sb("parts", [P, 3, H2, PARTS, D], BF16)
        qt = sb("qt", [P, H, N], BF16)
        kt = sb("kt", [P, H, N], BF16)
        v = sb("v", [P, NT, H, VW])
        a = sb("a", [P, RA, 2, 512])
        wq_f = a[:].rearrange("p r h n -> p (r h n)")[:, 0:KE * 3 * E].rearrange("p (k n) -> p k n", k=KE)
        work, t2, sq = (a[:].rearrange("p r h n -> p (r h n)")[:, lo * 2 * GT:hi * 2 * GT]
                        .rearrange("p (i h d) -> p i h d", h=H2, d=D) for lo, hi in ((RA - 5, RA - 2), (RA - 2, RA - 1), (RA - 1, RA)))
        rec = sb("rec", [P, 2, G, Q])
        ot = sb("ot", [P, 2, 512])
        at = a[:].rearrange("p r h n -> p (r h n)")[:, 0:NG * KE * GT].rearrange("p (g k n) -> p g k n", g=NG, k=KE)
        ao = parts[:].rearrange("p r h s d -> p (r h s d)")[:, 0:2 * NT * E].bitcast(F32).rearrange("p (i e) -> p i e", e=E)

        s_const = sem("s_const")
        s_made = sem("s_made")
        s_wsplit = sem("s_wsplit")
        s_xa = [sem(f"s_xa{g}") for g in range(NG)]
        s_xr = sem("s_xr")
        s_store = sem("s_store")
        s_st = sem("s_st")
        s_stat = sem("s_stat")
        s_eps = sem("s_eps")
        s_rstd = sem("s_rstd")
        s_xn = sem("s_xn")
        s_xT = sem("s_xT")
        s_xh = sem("s_xh")
        s_xl = sem("s_xl")
        s_qkv = sem("s_qkv")
        s_v = sem("s_v")
        s_d1 = sem("s_d1")
        s_add = sem("s_add")
        s_m = sem("s_m")
        s_u = sem("s_u")
        s_sq = sem("s_sq")
        s_var = sem("s_var")
        s_sd = sem("s_sd")
        s_r = sem("s_r")
        s_w = sem("s_w")
        s_sc = sem("s_sc")
        s_wb = sem("s_wb")
        s_h1 = sem("s_h1")
        s_r1 = sem("s_r1")
        s_h2 = sem("s_h2")
        s_parts = sem("s_parts")
        s_tr = sem("s_tr")
        s_ev = sem("s_ev")
        s_s = sem("s_s")
        s_q1 = sem("s_q1")
        s_a = sem("s_a")
        s_ad = sem("s_ad")
        s_ad1 = sem("s_ad1")
        s_passed = sem("s_passed")
        s_av = sem("s_av")
        s_rec = sem("s_rec")
        s_nrm = sem("s_nrm")
        s_ot = sem("s_ot")
        s_otT = sem("s_otT")
        s_aoT = sem("s_aoT")
        s_aT = sem("s_aT")
        s_y = sem("s_y")
        s_x1 = sem("s_x1")

        psT = lambda k: psum[:, k, :]
        psQK = lambda i: psum[:, 2 + i % 2, :].rearrange("p (h d) -> p h d", d=D)
        psV = psum[:, 4, 0:E]
        psTr = lambda c: psum[0:KP, 5 + c % 2, :].bitcast(BF16).rearrange("p (h t) -> p h t", h=8)
        S = lambda n: psum[:, 2 * (n % 3):2 * (n % 3) + 2, :]
        OT = lambda qc: psum[:, 6 + qc, :]

        LOWER = [(0, [(0, 0, range(0, 4))]),
                 (0, [(1, 0, range(1, 4)), (3, 384, range(3, 4))]),
                 (0, [(2, 0, range(2, 4))])]
        UPPER = [(1, [(j, 0, range(4, 8))]) for j in range(4)]
        CORNER = [(1, [(4, 0, range(4, 8))]),
                  (1, [(5, 0, range(5, 8)), (7, 384, range(7, 8))]),
                  (1, [(6, 0, range(6, 8))])]
        ORDER = [0, 2, 3, 1, 4, 8, 5, 9, 6, 7]
        UNITS = [(LOWER + UPPER + CORNER)[i] for i in ORDER]
        NU = len(UNITS)
        WORK = [(quad, u, half) for quad in range(H // Q) for u in range(NU) for half in range(2)]
        NB = len(WORK)
        width = lambda u: sum(len(o) * P for _, _, o in UNITS[u][1])
        diagonal = lambda u: UNITS[u][1][0][0] == UNITS[u][1][0][2][0]
        NDIAG = [sum(diagonal(u) for _, u, _ in WORK[:n]) for n in range(NB + 1)]
        LAST = [max(u for u in range(NU) if UNITS[u][0] == qc) for qc in range(2)]
        DONE = [n for n, (quad, u, half) in enumerate(WORK) if half and u in LAST]
        NQ = 2 * (H // Q)
        STEPS = NT + 6

        AOT = lambda g, k: psum[:, 5 + g + k, :]
        Y = lambda g, c: psum[:, ((7, 5), (5, 6))[g][c], :]

        def batches(engine, prepare, heads, finish):
            prepare(0, None)
            with engine.Fori(0, B - 1) as b:
                heads(b, True)
                prepare(b + 1, b)
            heads(B - 1, False)
            for g in range(NG):
                finish(B - 1, g)

        block = ctx.enter_context(nc.Block())

        @block.sync
        def _(sp):
            sp.sem_inc(s_store, ONE)
            for g in range(NG):
                sp.dma_start(xa[:, G * g:G * g + G, :], x[0, G * g:G * g + G, :, :].rearrange("t p e -> p t e")).then_inc(s_xa[g], 16)
            sp.dma_start(wq_f, w_qkv).then_inc(s_const, 16)
            sp.dma_start(ident[:], ident_in).then_inc(s_const, 16)
            sp.dma_start(wo[:], w_out).then_inc(s_const, 16)
            sp.dma_start(rope_sb[:], rope).then_inc(s_const, 16)
            sp.dma_start(affine[:], ln_affine.partition_broadcast(P)).then_inc(s_const, 16)
            def load_rows(b):
                for g in range(NG):
                    sp.dma_start(xa[:, G * g:G * g + G, :],
                                 x[bass.ds(b, 1), G * g:G * g + G, :, :].rearrange("o t p e -> p (o t) e")
                                 ).then_inc(s_xa[g], 16)

            def batch(b, more):
                if more:
                    sp.wait_ge(s_xn, ONE + NT * b + NT)
                    load_rows(b + 1)
                sp.wait_ge(s_store, ONE + 16 * b)
                sp.dma_start(xr[:], x[bass.ds(b, 1), :, :, :].rearrange("o t p e -> p (o t) e")).then_inc(s_xr, 16)
                sp.wait_ge(s_x1, ONE + 2 * NG * b + 2 * NG)
                sp.dma_start(x1[bass.ds(b, 1), :, :, :].rearrange("o t p e -> p (o t) e"), xr[:]).then_inc(s_store, 16)

            with sp.Fori(0, B - 1) as b:
                batch(b, True)
            batch(B - 1, False)
            sp.wait_ge(s_store, ONE + 16 * B)

        @block.gpsimd
        def _(pool):
            pool.memset(v[:, :, :, D + 1:], 0.0)
            pool.memset(v[:, :, :, D:D + 1], 1.0).then_inc(s_made, 1)
            pool.memset(neg_half[:], -0.5).then_inc(s_made, 1)
            pool.memset(eps[:], EPS).then_inc(s_made, 1)
            pool.memset(head_eps[:], EPS).then_inc(s_made, 1)
            pool.wait_ge(s_const, 80)
            pool.wait_ge(s_made, 4)

            def token_rstd(b, g):
                n = NG * b + g
                pool.wait_ge(s_stat, n + 1)
                r = rstd[:, G * g:G * g + G]
                pool.tensor_tensor(r, mv[:, G * g:G * g + G, 1], eps[:], ALU.add).then_inc(s_eps, 1)
                pool.wait_ge(s_eps, n + 1)
                pool.tensor_tensor(r, r, neg_half[:, 0:G], ALU.pow).then_inc(s_rstd, 1)

            def prepare(b, out):
                for s in range(STEPS):
                    if 0 <= (i := s - 3) < NT:
                        pool.wait_ge(s_w, NT * b + i + 1)
                        w = work[:, i % 6]
                        pool.tensor_tensor(w, w, affine[:, 0:1, :].to_broadcast([P, H2, D]), ALU.mult).then_inc(s_sc, 1)
                        pool.wait_ge(s_sc, NT * b + i + 1)
                        pool.tensor_tensor(w, w, affine[:, 1:2, :].to_broadcast([P, H2, D]), ALU.add).then_inc(s_wb, 1)
                    if (i := s) < NT:
                        pool.wait_ge(s_d1, NT * b + i + 1)
                        w = work[:, i % 6]
                        pool.tensor_tensor(w, w, t2[:, i % 2], ALU.add).then_inc(s_add, 1)

            def heads(b, more):
                if more:
                    for g in range(NG):
                        token_rstd(b + 1, g)
                for n, (quad, u, half) in enumerate(WORK):
                    if not diagonal(u):
                        continue
                    pool.wait_ge(s_q1, NB * b + n + 1)
                    two = len(UNITS[u][1])
                    d = a[:, n % RA].rearrange("p h (o q) -> p h o q", q=P)[:, :, 0:3 * two - 2:3, :]
                    pool.tensor_tensor(d, d, d, ALU.mult).then_inc(s_ad1, 1)
                    pool.wait_ge(s_ad1, NDIAG[NB] * b + NDIAG[n] + 1)
                    pool.sem_inc(s_passed, 1)
                    for k in range(two):
                        last = pool.affine_select(out=d[:, :, k], in_=d[:, :, k], compare_op=ALU.is_ge, fill=0.0,
                                                  base=0, pattern=[[0, 2], [1, P]], channel_multiplier=-1)
                    last.then_inc(s_ad, 1)

            for g in range(NG):
                token_rstd(0, g)
            batches(pool, prepare, heads, lambda b, g: None)

        @block.scalar
        def _(act):
            act.sem_inc(s_v, ONE)
            act.sem_inc(s_ev, ONE)
            act.wait_ge(s_const, 80)
            act.activation(ident_bf[:], ident[:], ACT.Copy).then_inc(s_wsplit, 1)
            act.activation(wq_h[:], wq_f, ACT.Copy).then_inc(s_wsplit, 1)
            act.wait_ge(s_made, 4)
            def keep_output(b, m):
                act.wait_ge(s_av, ONE + NB // 2 * b + (DONE[m] + 1) // 2)
                act.activation(ot[:, m % 2, :], OT(m % 2), ACT.Copy).then_inc(s_ot, 1)

            def transposed_out(b, g):
                for k in range(KE):
                    act.wait_ge(s_aoT, 4 * b + 2 * g + k + 1)
                    act.activation(at[:, g, k, :], AOT(g, k), ACT.Copy).then_inc(s_aT, 1)

            def finish(b, g):
                if g == 0:
                    keep_output(b, NQ - 1)
                transposed_out(b, g)

            def prepare(b, out):
                for s in range(STEPS):
                    if out is not None and s == 0:
                        keep_output(out, NQ - 1)
                    if s % G == 0 and s < NT:
                        g = s // G
                        for k in range(KE):
                            act.wait_ge(s_xT, 4 * b + 2 * g + k + 1)
                            act.activation(xh[:, g, k, :], psT(k), ACT.Copy).then_inc(s_xh, 1)
                    if (i := s) < NT:
                        act.wait_ge(s_qkv, NT * b + i + 1)
                        act.activation(v[:, i, :, 0:D], psV.rearrange("p (h d) -> p h d", d=D), ACT.Copy).then_inc(s_v, 1)
                    if 0 <= (i := s - 6) < NT:
                        for c in range(4):
                            act.wait_ge(s_tr, 4 * NT * b + 4 * i + c + 1)
                            to = (qt, kt)[c // 2]
                            act.activation(to[0:KP, 8 * (c % 2):8 * (c % 2) + 8, i * P:(i + 1) * P], psTr(c),
                                           ACT.Copy).then_inc(s_ev, 1)
                    if 0 <= (i := s - 2) < NT:
                        act.wait_ge(s_var, NT * b + i + 1)
                        act.activation(hr[:, i], var[:, i], ACT.Sqrt, bias=head_eps[:], scale=1.0 / D).then_inc(s_sd, 1)
                    if 0 <= (i := s - 4) < NT:
                        act.wait_ge(s_r1, NT * b + i + 1)
                        act.activation(parts[:, i % 3, :, 1, :], work[:, i % 6], ACT.Copy).then_inc(s_h2, 1)
                    if 0 <= (i := s - 3) < NT:
                        act.wait_ge(s_wb, NT * b + i + 1)
                        act.activation(parts[:, i % 3, :, 0, :], work[:, i % 6], ACT.Copy).then_inc(s_h1, 1)
                    if 0 <= (i := s - 1) < NT:
                        act.wait_ge(s_u, NT * b + i + 1)
                        if i >= 2:
                            act.wait_ge(s_var, NT * b + i - 1)
                        act.activation(sq[:, i % 2], work[:, i % 6], ACT.Square).then_inc(s_sq, 1)
                    if out is not None and s in (0, 2):
                        transposed_out(out, s // 2)

            def heads(b, more):
                m = 0
                for n, (quad, u, half) in enumerate(WORK):
                    act.wait_ge(s_s, NB * b + n + 1)
                    act.wait_ge(s_av, ONE + NB // 2 * b + max(0, (n - RA) // 2 + 1))
                    w = width(u)
                    act.activation(a[:, n % RA, :, 0:w], S(n)[:, :, 0:w], ACT.Square).then_inc(s_q1, 1)
                    if n - LAG in DONE:
                        keep_output(b, m)
                        m += 1

            batches(act, prepare, heads, finish)

        @block.vector
        def _(dve):
            for free in (s_xn, s_xl, s_nrm, s_x1):
                dve.sem_inc(free, ONE)
            dve.wait_ge(s_wsplit, 2)
            dve.tensor_tensor(wq_l[:], wq_f, wq_h[:].bitcast(F32), ALU.subtract).then_inc(s_wsplit, 1)

            def normalise(b, g):
                n = NG * b + g
                dve.wait_ge(s_xa[g], 16 * b + 16)
                for t in range(G * g, G * g + G):
                    dve.bn_stats(stats[:, t, :], xa[:, t, :]).then_inc(s_st, 1)
                dve.wait_ge(s_st, NT * b + G * g + G)
                dve.memset(pad[:], 0.0)
                for t in range(G * g, G * g + G):
                    last = dve.bn_aggr(mv[:, t, :], stats[:, t, :])
                last.then_inc(s_stat, 1)

            def normalise2(b, g):
                dve.wait_ge(s_rstd, NG * b + g + 1)
                for t in range(G):
                    i = G * g + t
                    dve.tensor_scalar(xn[:, g, t, :], xa[:, i, :], mv[:, i, 0:1], rstd[:, i:i + 1],
                                      ALU.subtract, ALU.mult).then_inc(s_xn, 1)

            def norm(b, m):
                quad, qc = m // 2, m % 2
                dve.wait_ge(s_otT, NQ * b + m + 1)
                o = OT(qc).rearrange("p (i h d) -> p i h d", h=Q, d=VW)
                r = rec[:, qc]
                dve.reciprocal(r, o[:, :, :, D]).then_inc(s_rec, 1)
                dve.wait_ge(s_rec, NQ * b + m + 1)
                to = ao[:, G * qc:G * qc + G, Q * D * quad:Q * D * quad + Q * D].rearrange("p i (h d) -> p i h d", d=D)
                dve.tensor_tensor(to, o[:, :, :, 0:D], r.unsqueeze(3).to_broadcast([P, G, Q, D]),
                                  ALU.mult).then_inc(s_nrm, 1)

            def finish(b, g):
                if g == 0:
                    dve.wait_ge(s_xr, 16 * b + 16)
                for c in range(2):
                    dve.wait_ge(s_y, 4 * b + 2 * g + c + 1)
                    t = xr[:, G * g + 2 * c:G * g + 2 * c + 2, :]
                    dve.tensor_tensor(t, t, Y(g, c).rearrange("p (t e) -> p t e", e=E), ALU.add).then_inc(s_x1, 1)

            def last_norm_and_finish(b, g):
                if g == 0:
                    norm(b, NQ - 1)
                finish(b, g)

            def prepare(b, out):
                for s in range(STEPS):
                    if out is not None and s == 0:
                        norm(out, NQ - 1)
                    if s % G == 0 and s < NT:
                        g = s // G
                        for k in range(KE):
                            dve.wait_ge(s_xh, 4 * b + 2 * g + k + 1)
                            dve.tensor_tensor(xl[:, g, k, :], psT(k), xh[:, g, k, :].bitcast(F32),
                                              ALU.subtract).then_inc(s_xl, 1)
                    if 0 <= (i := s - 3) < NT:
                        w = work[:, i % 6]
                        dve.wait_ge(s_sd, NT * b + i + 1)
                        dve.reciprocal(hr[:, i], hr[:, i]).then_inc(s_r, 1)
                        dve.wait_ge(s_r, NT * b + i + 1)
                        dve.tensor_tensor(w, w, hr[:, i].unsqueeze(2).to_broadcast([P, H2, D]), ALU.mult).then_inc(s_w, 1)
                    if 0 <= (i := s - 4) < NT:
                        w = work[:, i % 6]
                        dve.wait_ge(s_h1, NT * b + i + 1)
                        dve.tensor_tensor(w, w, parts[:, i % 3, :, 0, :], ALU.subtract).then_inc(s_r1, 1)
                    if (i := s) < NT:
                        dve.wait_ge(s_qkv, NT * b + i + 1)
                        qk = psQK(i)
                        w, t = work[:, i % 6], t2[:, i % 2]
                        hd = D // 2
                        dve.tensor_tensor(w, qk, rope_sb[:, 0, i:i + 1, :].to_broadcast([P, H2, D]), ALU.mult)
                        dve.tensor_tensor(t[:, :, 0:hd], qk[:, :, hd:D],
                                          rope_sb[:, 1, i:i + 1, 0:hd].to_broadcast([P, H2, hd]), ALU.mult)
                        dve.tensor_tensor(t[:, :, hd:D], qk[:, :, 0:hd],
                                          rope_sb[:, 1, i:i + 1, hd:D].to_broadcast([P, H2, hd]), ALU.mult
                                          ).then_inc(s_d1, 1)
                    if 0 <= (i := s - 2) < NT:
                        dve.wait_ge(s_sq, NT * b + i + 1)
                        dve.reduce_sum(var[:, i], sq[:, i % 2], AX.X).then_inc(s_var, 1)
                    if 0 <= (i := s - 5) < NT:
                        w, q, k = work[:, i % 6], parts[:, i % 3, 0:H], parts[:, i % 3, H:H2]
                        dve.wait_ge(s_h2, NT * b + i + 1)
                        dve.tensor_tensor(q[:, :, 5, :], w[:, 0:H], q[:, :, 1, :], ALU.subtract)
                        dve.tensor_tensor(k[:, :, 4, :], w[:, H:H2], k[:, :, 1, :], ALU.subtract)
                        dve.tensor_copy(q[:, :, 2, :], q[:, :, 0, :])
                        dve.tensor_copy(q[:, :, 4, :], q[:, :, 0, :])
                        dve.tensor_copy(q[:, :, 3, :], q[:, :, 1, :])
                        dve.tensor_copy(k[:, :, 3, :], k[:, :, 0, :])
                        dve.tensor_copy(k[:, :, 5, :], k[:, :, 0, :])
                        dve.tensor_copy(k[:, :, 2, :], k[:, :, 1, :]).then_inc(s_parts, 1)
                    if 0 <= (i := s - 1) < NT:
                        w = work[:, i % 6]
                        dve.wait_ge(s_add, NT * b + i + 1)
                        dve.reduce_sum(mean[:, i], w, AX.X).then_inc(s_m, 1)
                        dve.wait_ge(s_m, NT * b + i + 1)
                        dve.scalar_tensor_tensor(out=w, in0=mean[:, i].unsqueeze(2).to_broadcast([P, H2, D]),
                                                 scalar=-1.0 / D, in1=w, op0=ALU.mult, op1=ALU.add).then_inc(s_u, 1)
                    if out is not None and s in (1, 3):
                        finish(out, s // 2)

            def heads(b, more):
                if more:
                    for g in range(NG):
                        normalise(b + 1, g)
                    for g in range(NG):
                        normalise2(b + 1, g)
                m = 0
                for n, (quad, u, half) in enumerate(WORK):
                    lo = P if diagonal(u) else 0
                    hi = UNITS[u][1][1][1] if len(UNITS[u][1]) > 1 else width(u)
                    dve.wait_ge(s_q1, NB * b + n + 1)
                    t = a[:, n % RA, :, lo:hi]
                    dve.tensor_tensor(t, t, t, ALU.mult).then_inc(s_a, 1)
                    if n - LAG - 3 in DONE:
                        norm(b, m)
                        m += 1

            for g in range(NG):
                normalise(0, g)
            for g in range(NG):
                normalise2(0, g)
            batches(dve, prepare, heads, last_norm_and_finish)

        @block.tensor
        def _(pe):
            pe.sem_inc(s_av, ONE)
            pe.wait_ge(s_wsplit, 3)

            def project(i, g, t):
                for out, lo, hi in ((psum[:, 2 + i % 2, :], 0, 2 * E), (psV, 2 * E, 3 * E)):
                    n = 0
                    for xs, ws in ((xh, wq_h), (xh, wq_l), (xl, wq_h)):
                        for k in range(KE):
                            last = pe.matmul(out, xs[:, g, k, t * P:(t + 1) * P], ws[:, k, lo:hi],
                                             start=n == 0, stop=n == 3 * KE - 1)
                            n += 1
                last.then_inc(s_qkv, 1)

            def outputs(b, m):
                pe.wait_ge(s_ot, NQ * b + m + 1)
                for i in range(G):
                    last = pe.transpose(OT(m % 2)[:, i * P:(i + 1) * P], ot[:, m % 2, i * P:(i + 1) * P], ident[:])
                last.then_inc(s_otT, 1)

            def transpose_out(b, g):
                pe.wait_ge(s_nrm, ONE + NQ * b + NQ - 1 + g)
                for k in range(KE):
                    if g:
                        pe.wait_ge(s_x1, ONE + 4 * b + 2)
                    for t in range(G):
                        last = pe.transpose(AOT(g, k)[:, t * P:(t + 1) * P], ao[:, G * g + t, k * P:(k + 1) * P], ident[:])
                    last.then_inc(s_aoT, 1)

            def project_out(b, g):
                if g == 0:
                    pe.wait_ge(s_nrm, ONE + NQ * b + NQ)
                pe.wait_ge(s_aT, 4 * b + 2 * g + 2)
                for t in range(G):
                    for k in range(KE):
                        last = pe.matmul(Y(g, t // 2)[:, (t % 2) * E:(t % 2) * E + E], at[:, g, k, t * P:(t + 1) * P],
                                         wo[:, k, :], start=k == 0, stop=k == KE - 1)
                    if t % 2:
                        last.then_inc(s_y, 1)

            def finish(b, g):
                transpose_out(b, g)
                if g == 0:
                    outputs(b, NQ - 1)
                project_out(b, g)

            def prepare(b, out):
                for s in range(STEPS):
                    if s % G == 0 and s < NT:
                        g = s // G
                        pe.wait_ge(s_xn, ONE + NT * b + G * g + G)
                        pe.wait_ge(s_xl, ONE + 4 * b + 2 * g)
                        for k in range(KE):
                            for t in range(G):
                                last = pe.transpose(psT(k)[:, t * P:(t + 1) * P], xn[:, g, t, k * P:(k + 1) * P], ident[:])
                            last.then_inc(s_xT, 1)
                        if out is not None and s == 0:
                            transpose_out(out, 0)
                            outputs(out, NQ - 1)
                        pe.wait_ge(s_xl, ONE + 4 * b + 2 * g + 2)
                    if (i := s) < NT:
                        if i >= 2:
                            pe.wait_ge(s_d1, NT * b + i - 1)
                        pe.wait_ge(s_v, ONE + NT * b + i)
                        project(i, i // G, i % G)
                    if out is not None and s == 2:
                        transpose_out(out, 1)
                    if out is not None and s in (1, 3):
                        project_out(out, s // 2)
                    if 0 <= (i := s - 6) < NT:
                        pe.wait_ge(s_parts, NT * b + i + 1)
                        if i == 0:
                            pe.wait_ge(s_x1, ONE + 4 * b)
                        for c in range(4):
                            if i or c:
                                pe.wait_ge(s_ev, ONE + 4 * NT * b + 4 * i + c - 1)
                            for h in range(8):
                                last = pe.transpose(psTr(c)[:, h, :], parts[:, i % 3, 8 * c + h], ident_bf[:])
                            last.then_inc(s_tr, 1)
            def heads(b, more):
                pe.wait_ge(s_ev, ONE + 4 * NT * b + 4 * NT)
                pe.wait_ge(s_v, ONE + NT * b + NT)

                def scores(n):
                    quad, u, half = WORK[n]
                    if n >= 3:
                        pe.wait_ge(s_q1, NB * b + n - 2)
                    for hh in range(2):
                        h = Q * quad + 2 * half + hh
                        for j, col, tiles in UNITS[u][1]:
                            w = len(tiles) * P
                            last = pe.matmul(S(n)[:, hh, col:col + w], kt[0:KP, h, j * P:(j + 1) * P],
                                             qt[0:KP, h, tiles[0] * P:tiles[0] * P + w], start=True, stop=True)
                    last.then_inc(s_s, 1)

                def values(n):
                    quad, u, _ = WORK[n]
                    qc = UNITS[u][0]
                    pe.wait_ge(s_a, NB * b + n + 1)
                    if diagonal(u):
                        pe.wait_ge(s_ad, NDIAG[NB] * b + NDIAG[n + 1])
                    if UNITS[u][1][0][0] == 0:
                        pe.wait_ge(s_nrm, ONE + NQ * b + max(0, 2 * quad + qc - 1))
                    for j, col, tiles in UNITS[u][1]:
                        w = len(tiles) * P
                        at_ = (tiles[0] - 4 * qc) * P
                        for hh in range(Q):
                            last = pe.matmul(OT(qc)[VW * hh:VW * hh + VW, at_:at_ + w], v[:, j, Q * quad + hh, :],
                                             a[:, (n - 1 + hh // 2) % RA, hh % 2, col:col + w],
                                             start=j == 0, stop=j == 4 * qc + 3, skip_group_check=True)
                    last.then_inc(s_av, 1)

                m = 0
                for n in range(NB + LAG):
                    if n < NB:
                        scores(n)
                    if n > LAG and (n - LAG) % 2:
                        values(n - LAG)
                    if n - LAG - 3 in DONE:
                        outputs(b, m)
                        m += 1

            batches(pe, prepare, heads, finish)


def feed_forward(nc, x1, w1, w2, gate, taps_in, select_in, ident_in, x3, out):
    ctx = ExitStack()
    with ctx:
        def sb(name, shape, dt=F32):
            return ctx.enter_context(nc.sbuf_tensor(name, shape, dt))

        def sem(name):
            return ctx.enter_context(nc.semaphore(name))

        psum = ctx.enter_context(nc.psum_tensor("ffn_psum", [P, 8, 512], F32))
        TT = 2 * NT
        TOK = B * P
        CR = 32

        w1h = sb("w1h", [P, FC, KE, 2, P], F32R)
        w1l = sb("w1l", [P, FC, KE, 2, P], F32R)
        w2h = sb("w2h", [P, FC, E], F32R)
        w2l = sb("w2l", [P, FC, E], F32R)
        GW = KE * NX + P - NX
        gt_h = sb("gt_h", [P, GW], F32R)
        gt_l = sb("gt_l", [P, GW], F32R)
        ident = sb("f_ident", [P, P])
        ident_bf = sb("f_ident_bf", [P, P], BF16)
        select = sb("select_sb", [3 * CR, FM, P], BF16)
        taps = sb("taps_sb", [P, LAGS, E])
        xp = sb("xp", [P, B, E])
        xe = sb("xe", [P, B, E])
        back = sb("back", [P, B * E])
        z = sb("z", [P, B, E])
        tmp = sb("tmp", [P, E])
        xh = sb("f_xh", [P, 2, KE, TOK], F32R)
        xl = sb("f_xl", [P, 2, KE, TOK], F32R)
        pr = sb("pr", [P, TOK])
        ah = sb("ah", [P, 2, TOK], F32R)
        al = sb("al", [P, 2, TOK], F32R)
        combT = sb("combT", [3 * CR, TOK], BF16)
        stats = sb("f_stats", [P, 2, B, 6])
        mv = sb("f_mv", [P, 2, B, 2])
        rstd = sb("f_rstd", [P, 2, B])
        eps = sb("f_eps", [P, B])
        neg_half = sb("f_half", [P, B])
        pad = sb("f_pad", [P, 1])
        mx = sb("mx", [P, B])
        rest = sb("rest", [P, B, NX + 2])
        lg = rest[:, :, 0:NX]
        prob = sb("prob", [P, B, NX + 2])
        top = sb("top", [P, B, 8])
        comb = prob[:, :, 0:NX]
        comb3 = sb("comb3", [P, B, 3, CR], BF16)
        tw = z[:].rearrange("p a b -> p (a b)")[:, 0:8 * 16].rearrange("p (s h n) -> p s h n", s=4, h=KE)
        kcol = top[:].rearrange("p b n -> p (b n)")[:, 0:LAGS * KE].rearrange("p (m k) -> p m k", k=KE)

        names = """const made wh wl gsplit taps_a taps_v taps_d taps_p pst peps prs pxn tx xh xl
                   lgT lgS lgX sm ex comb3 cx cT g u cb silu p1 p ah al s2 oT back x2 cst ceps crs cy plink clink mx
                   conv_link csilu x3 xp xe store link""".split()
        s = {n: sem("f_" + n) for n in names}
        s_wst = [sem("f_wst0"), sem("f_wst1")]

        GB = lambda q: psum[:, 2 * (q % 2), :]
        UB = lambda q: psum[:, 2 * (q % 2) + 1, :]
        CB = psum[:, 4, :]
        OB = lambda m: psum[:, 5 + m, :]
        X = psum[:, 7, :]
        stage1 = xe[:].rearrange("p b e -> p (b e)").rearrange("p (i n) -> p i n", i=2)
        stage2 = back[:].rearrange("p (i n) -> p i n", i=4)
        halves = psum[:, 0:2, :].rearrange("p a (l e) -> p (a l) e", e=E)
        backT = back[:].rearrange("p (m n) -> p m n", m=KE)
        backY = back[:].rearrange("p (b e) -> p b e", e=E)
        zT = z[:].rearrange("p b e -> p (b e)")[:, 0:TOK]

        def tiles(engine, tile):
            tile(0, 0, None, True)
            tile(1, 1, "conv", True)
            with engine.Fori(1, NT // 2) as i:
                tile(2 * i, 0, "conv", True)
                tile(2 * i + 1, 1, "conv", True)
            tile(NT, 0, "conv", True)
            tile(NT + 1, 1, "plain", True)
            with engine.Fori(NT // 2 + 1, NT - 1) as i:
                tile(2 * i, 0, "plain", True)
                tile(2 * i + 1, 1, "plain", True)
            tile(TT - 2, 0, "plain", True)
            tile(TT - 1, 1, "plain", False)

        first = lambda n: isinstance(n, int) and n == 0

        block = ctx.enter_context(nc.Block())

        @block.sync
        def _(sp):
            def rows(dram, t):
                return dram[:, bass.ds(t, 1), :, :].rearrange("b o p e -> p (b o) e")

            def load(to, n, second, name):
                sp.dma_start(to[:], rows(x3, n - NT) if second else rows(x1, n)).then_inc(s[name], 16)

            sp.sem_inc(s["store"], ONE)
            sp.dma_start(ident[:], ident_in).then_inc(s["const"], 16)
            sp.dma_start(z[:].rearrange("p b e -> p (b e)")[:, 0:4 * KE * 16], taps_in).then_inc(s["const"], 16)
            sp.dma_start(pr[:, 0:GW], gate).then_inc(s["const"], 16)
            sp.dma_start(select[:], select_in).then_inc(s["const"], 16)
            load(xp, 0, False, "xp")
            for c in range(FC):
                if c >= 2:
                    sp.wait_ge(s["wl"], 2 * (c - 1))
                sp.dma_start(stage1[:, c % 2, :], w1[:, c]).then_inc(s_wst[c % 2], 16)
                sp.dma_start(stage2[:, c % 2, :], w2[:, c]).then_inc(s_wst[c % 2], 16)
                if c == 4:
                    sp.wait_ge(s["tx"], KE)
                    load(xp, 1, False, "xp")
            sp.wait_ge(s["wl"], 2 * FC)

            def turn(n, loads_second, residual_second, store_to, prologue):
                if prologue:
                    sp.wait_ge(s["tx"], KE * (n + 1))
                    load(xp, n + 1, loads_second, "xp")
                sp.wait_ge(s["store"], ONE + 16 * (n - 1))
                load(xe, n - 1, residual_second, "xe")
                if store_to is x3:
                    sp.wait_ge(s["x3"], n)
                    sp.dma_start(rows(x3, n - 1), xe[:]).then_inc(s["store"], 16)
                else:
                    sp.wait_ge(s["x2"], 2 * n)
                    sp.dma_start(rows(out, n - 1 - NT), xe[:]).then_inc(s["store"], 16)

            with sp.Fori(1, NT - 1) as n:
                turn(n, False, False, x3, True)
            turn(NT - 1, True, False, x3, True)
            turn(NT, True, False, x3, True)
            with sp.Fori(NT + 1, TT - 1) as n:
                turn(n, True, True, out, True)
            turn(TT - 1, True, True, out, False)
            turn(TT, True, True, out, False)
            sp.wait_ge(s["store"], ONE + 16 * TT)

        @block.gpsimd
        def _(pool):
            pool.memset(eps[:], EPS).then_inc(s["made"], 1)
            pool.memset(neg_half[:], -0.5).then_inc(s["made"], 1)
            pool.memset(prob[:, :, NX:NX + 1], -1.0).then_inc(s["made"], 1)
            pool.memset(prob[:, :, NX + 1:], -2.0).then_inc(s["made"], 1)
            pool.memset(comb3[:], 0.0).then_inc(s["made"], 1)
            pool.memset(tmp[:, 0:P], 1.0).then_inc(s["made"], 1)
            pool.wait_ge(s["made"], 6)

            def rstd_of(which, ready, added, done, m):
                pool.wait_ge(s[ready], m + 1)
                r = rstd[:, which]
                pool.tensor_tensor(r, mv[:, which, :, 1], eps[:], ALU.add).then_inc(s[added], 1)
                pool.wait_ge(s[added], m + 1)
                pool.tensor_tensor(r, r, neg_half[:], ALU.pow).then_inc(s[done], 1)

            def convolve(e):
                pool.wait_ge(s["cy"], e + 1)
                links = e * CONV_LINKS
                for l in range(B):
                    pool.tensor_tensor(z[:, l], backY[:, l], taps[:, 0], ALU.mult).then_inc(s["conv_link"], 1)
                    links = links + 1
                for m in range(1, LAGS):
                    for l in range(m, B):
                        pool.wait_ge(s["conv_link"], links)
                        pool.tensor_tensor(tmp[:], backY[:, l - m], taps[:, m], ALU.mult).then_inc(s["conv_link"], 1)
                        links = links + 1
                        pool.wait_ge(s["conv_link"], links)
                        last = pool.tensor_tensor(z[:, l], z[:, l], tmp[:], ALU.add)
                        last.then_inc(s["conv_link"], 1)
                        links = links + 1

            rstd_of(0, "pst", "peps", "prs", 0)

            def tile(n, parity, epilogue, prologue):
                if epilogue == "conv":
                    rstd_of(1, "cst", "ceps", "crs", n - 1)
                if prologue:
                    rstd_of(0, "pst", "peps", "prs", n + 1)
                if epilogue == "conv":
                    convolve(n - 1)

            tiles(pool, tile)

        @block.scalar
        def _(act):
            act.wait_ge(s["const"], 64)
            act.activation(ident_bf[:], ident[:], ACT.Copy).then_inc(s["gsplit"], 1)
            act.activation(gt_h[:], pr[:, 0:GW], ACT.Copy).then_inc(s["gsplit"], 1)
            act.activation(tw[:, 0:2], tw[:, 0:2], ACT.Sigmoid).then_inc(s["taps_a"], 1)
            act.wait_ge(s["taps_p"], 1)
            act.activation(taps[:], halves, ACT.Copy).then_inc(s["taps_a"], 1)

            def split(c):
                act.wait_ge(s_wst[c % 2], 32 * (c // 2) + 32)
                act.activation(w1h[:, c].rearrange("p k g f -> p (k g f)"), stage1[:, c % 2, :], ACT.Copy).then_inc(s["wh"], 1)
                act.activation(w2h[:, c], stage2[:, c % 2, :], ACT.Copy).then_inc(s["wh"], 1)

            def high(m, parity, k):
                act.wait_ge(s["tx"], KE * m + k + 1)
                act.activation(xh[:, parity, k], X, ACT.Copy).then_inc(s["xh"], 1)

            def logits(m, conv):
                act.wait_ge(s["lgT"], m + 1)
                if conv is not None:
                    act.wait_ge(s["x3"], conv)
                act.activation(zT, X, ACT.Copy).then_inc(s["lgS"], 1)

            def exps(m):
                act.wait_ge(s["sm"], m + 1)
                act.activation(lg, lg, ACT.Exp).then_inc(s["ex"], 1)

            def weights(m):
                act.wait_ge(s["cx"], m + 1)
                act.activation(combT[:], X.bitcast(BF16)[0:3 * CR, 0:TOK], ACT.Copy).then_inc(s["cT"], 1)

            def silu(n, q, c):
                act.wait_ge(s["g"], FC * n + c + 1)
                act.wait_ge(s["al"], FC * n + c)
                act.activation(pr[:], GB(q), ACT.Silu).then_inc(s["silu"], 1)

            def high_act(n, q, c):
                act.wait_ge(s["p"], FC * n + c + 1)
                act.activation(ah[:, q % 2], pr[:], ACT.Copy).then_inc(s["ah"], 1)

            def outputs(e):
                act.wait_ge(s["s2"], FC * (e + 1))
                for m in range(KE):
                    act.activation(backT[:, m], OB(m), ACT.Copy).then_inc(s["oT"], 1)

            split(0)
            for k in range(KE):
                high(0, 0, k)
            logits(0, None)
            exps(0)
            weights(0)
            split(1)
            silu(0, 0, 0)

            def tile(n, parity, epilogue, prologue):
                if epilogue:
                    outputs(n - 1)
                for c in range(1, FC):
                    q = FC * parity + c
                    if first(n) and c + 1 < FC:
                        split(c + 1)
                    high_act(n, q - 1, c - 1)
                    silu(n, q, c)
                    if epilogue == "conv" and c == 14:
                        act.wait_ge(s["conv_link"], n * CONV_LINKS)
                        act.activation(z[:], z[:], ACT.Silu).then_inc(s["csilu"], 1)
                    if prologue:
                        if c in (12, 14):
                            high(n + 1, 1 - parity, (c - 12) // 2)
                        if c == 17:
                            logits(n + 1, n if epilogue == "conv" else None)
                        if c == 19:
                            exps(n + 1)
                        if c == 24:
                            weights(n + 1)
                high_act(n, FC * parity + FC - 1, FC - 1)
                if prologue:
                    silu(n + 1, FC * parity + FC, 0)

            tiles(act, tile)
            outputs(TT - 1)

        @block.vector
        def _(dve):
            dve.wait_ge(s["gsplit"], 2)
            dve.tensor_tensor(gt_l[:], pr[:, 0:GW],
                              gt_h[:].bitcast(F32), ALU.subtract).then_inc(s["gsplit"], 1)
            sd, sa, be, ga = (tw[:, i] for i in range(4))
            v = [0]

            def step(ins):
                v[0] += 1
                ins.then_inc(s["taps_v"], 1)
                dve.wait_ge(s["taps_v"], v[0])

            dve.wait_ge(s["taps_a"], 1)
            step(dve.tensor_tensor(sa, sd, sa, ALU.mult))
            step(dve.tensor_tensor(be, be, ga, ALU.mult))
            step(dve.tensor_tensor(be, be, sa, ALU.mult))
            step(dve.tensor_scalar(be, be, float(1.0 / 16) ** 0.5, None, ALU.mult))
            step(dve.tensor_scalar(sa, sa, -1.0, 1.0, ALU.mult, ALU.add))
            for m in range(LAGS):
                step(dve.reduce_sum(kcol[:, m], be, AX.X))
                if m < LAGS - 1:
                    step(dve.tensor_tensor(be, be, sa, ALU.mult))
            zd = z[:].rearrange("p b e -> p (b e)").rearrange("p (m k n) -> p m k n", m=LAGS, k=KE)
            for m in range(LAGS):
                for k in range(KE):
                    last = dve.tensor_scalar(zd[:, m, k], ident[:], kcol[:, m, k:k + 1], None, ALU.mult)
            last.then_inc(s["taps_d"], 1)

            def split(c):
                dve.wait_ge(s["wh"], 2 * c + 2)
                dve.tensor_tensor(w1l[:, c].rearrange("p k g f -> p (k g f)"), stage1[:, c % 2, :],
                                  w1h[:, c].bitcast(F32).rearrange("p k g f -> p (k g f)"), ALU.subtract).then_inc(s["wl"], 1)
                dve.tensor_tensor(w2l[:, c], stage2[:, c % 2, :], w2h[:, c].bitcast(F32), ALU.subtract).then_inc(s["wl"], 1)

            def aggregate(which, done):
                for b in range(B):
                    last = dve.bn_aggr(mv[:, which, b], stats[:, which, b])
                last.then_inc(s[done], 1)

            def wait_apart(name, value):
                dve.wait_ge(s[name], value)
                dve.memset(pad[:], 0.0)

            def normalise(which, rows, to, ready, done, m):
                dve.wait_ge(s[ready], m + 1)
                for b in range(B):
                    last = dve.tensor_scalar(to[:, b], rows[:, b], mv[:, which, b, 0:1], rstd[:, which, b:b + 1],
                                             ALU.subtract, ALU.mult)
                last.then_inc(s[done], 1)

            def prologue_stats(m):
                dve.wait_ge(s["xp"], 16 * m + 16)
                for b in range(B):
                    last = dve.bn_stats(stats[:, 0, b], xp[:, b])
                last.then_inc(s["plink"], 1)
                wait_apart("plink", m + 1)
                aggregate(0, "pst")

            def low(m, parity, k):
                dve.wait_ge(s["xh"], KE * m + k + 1)
                dve.tensor_tensor(xl[:, parity, k], X, xh[:, parity, k].bitcast(F32), ALU.subtract).then_inc(s["xl"], 1)

            def softmax(m):
                L = X.rearrange("p (b n) -> p b n", n=P)[:, :, 0:NX]
                dve.wait_ge(s["lgX"], m + 1)
                dve.reduce_max(mx[:], L, AX.X).then_inc(s["mx"], 1)
                dve.wait_ge(s["mx"], m + 1)
                dve.tensor_tensor(lg, L, mx[:].unsqueeze(2).to_broadcast([P, B, NX]), ALU.subtract).then_inc(s["sm"], 1)

            def link(m, k, ins, apart=False):
                ins.then_inc(s["link"], 1)
                (wait_apart if apart else lambda a, v: dve.wait_ge(s[a], v))("link", m * ROUTE_LINKS + k)

            pb = prob[:, :, 0:NX]

            def probabilities(m):
                dve.wait_ge(s["ex"], m + 1)
                link(m, 1, dve.reduce_sum(mx[:], lg, AX.X))
                link(m, 2, dve.reciprocal(mx[:], mx[:]))
                link(m, 3, dve.tensor_tensor(pb, lg, mx[:].unsqueeze(2).to_broadcast([P, B, NX]), ALU.mult), True)
                for b in range(B):
                    last = dve.max(top[:, b], prob[:, b, 0:NX])
                link(m, 4, last)
                dve.tensor_copy(top[:, :, TOPK:8], prob[:, :, NX:NX + 2]).then_inc(s["link"], 1)

            def choose(m):
                wait_apart("link", m * ROUTE_LINKS + 5)
                for b in range(B):
                    last = dve.match_replace(rest[:, b], top[:, b], prob[:, b], 0.0)
                link(m, 6, last)
                link(m, 7, dve.tensor_tensor(comb, pb, rest[:, :, 0:NX], ALU.subtract))
                link(m, 8, dve.tensor_copy(comb3[:, :, 0, 0:NX], comb))
                link(m, 9, dve.tensor_tensor(comb, comb, comb3[:, :, 0, 0:NX], ALU.subtract))
                link(m, 10, dve.tensor_copy(comb3[:, :, 1, 0:NX], comb))
                dve.tensor_tensor(comb3[:, :, 2, 0:NX], comb, comb3[:, :, 1, 0:NX], ALU.subtract).then_inc(s["comb3"], 1)

            def product(n, q, c):
                t = pr[:]
                dve.wait_ge(s["silu"], FC * n + c + 1)
                dve.wait_ge(s["u"], FC * n + c + 1)
                if c < FM:
                    dve.tensor_tensor(t, t, UB(q), ALU.mult).then_inc(s["p1"], 1)
                    dve.wait_ge(s["p1"], FM * n + c + 1)
                    dve.wait_ge(s["cb"], FM * n + c + 1)
                    dve.tensor_tensor(t, t, CB, ALU.mult).then_inc(s["p"], 1)
                else:
                    dve.tensor_tensor(t, t, UB(q), ALU.mult).then_inc(s["p"], 1)

            def low_act(n, q, c):
                dve.wait_ge(s["ah"], FC * n + c + 1)
                dve.tensor_tensor(al[:, q % 2], pr[:], ah[:, q % 2].bitcast(F32), ALU.subtract).then_inc(s["al"], 1)

            def residual(e, half):
                if half == 0:
                    dve.wait_ge(s["xe"], 16 * e + 16)
                dve.wait_ge(s["back"], 2 * e + half + 1)
                t = xe[:, 2 * half:2 * half + 2]
                dve.tensor_tensor(t, t, X.rearrange("p (b e) -> p b e", e=E), ALU.add).then_inc(s["x2"], 1)

            split(0)
            prologue_stats(0)
            normalise(0, xp, xp, "prs", "pxn", 0)
            for k in range(KE):
                low(0, 0, k)
            softmax(0)
            probabilities(0)
            choose(0)
            split(1)
            product(0, 0, 0)

            def tile(n, parity, epilogue, prologue):
                for c in range(1, FC):
                    q = FC * parity + c
                    if first(n) and c + 1 < FC:
                        split(c + 1)
                    low_act(n, q - 1, c - 1)
                    product(n, q, c)
                    if epilogue and c in (4, 6):
                        residual(n - 1, (c - 4) // 2)
                    if epilogue == "conv":
                        if c == 7:
                            dve.wait_ge(s["x2"], 2 * n)
                            for b in range(B):
                                last = dve.bn_stats(stats[:, 1, b], xe[:, b])
                            last.then_inc(s["clink"], 1)
                            wait_apart("clink", n)
                            aggregate(1, "cst")
                        if c == 8:
                            normalise(1, xe, backY, "crs", "cy", n - 1)
                        if c == 15:
                            dve.wait_ge(s["csilu"], n)
                            dve.tensor_tensor(xe[:], xe[:], z[:], ALU.add).then_inc(s["x3"], 1)
                    if prologue:
                        if c == 9:
                            prologue_stats(n + 1)
                        if c == 10:
                            normalise(0, xp, xp, "prs", "pxn", n + 1)
                        if c in (12, 14):
                            low(n + 1, 1 - parity, (c - 12) // 2)
                        if c == 19:
                            softmax(n + 1)
                        if c == 20:
                            probabilities(n + 1)
                        if c == 21:
                            choose(n + 1)
                low_act(n, FC * parity + FC - 1, FC - 1)
                if prologue:
                    product(n + 1, FC * parity + FC, 0)

            tiles(dve, tile)
            for half in range(2):
                residual(TT - 1, half)

        @block.tensor
        def _(pe):
            pe.wait_ge(s["taps_d"], 1)
            pe.wait_ge(s["made"], 6)
            zd = z[:].rearrange("p b e -> p (b e)")
            for m in range(LAGS):
                for k in range(KE):
                    at_ = (m * KE + k) * P
                    last = pe.matmul(halves[:, m, k * P:(k + 1) * P], tmp[:, 0:P], zd[:, at_:at_ + P], start=True, stop=True)
            last.then_inc(s["taps_p"], 1)
            pe.wait_ge(s["gsplit"], 3)

            def three(out, lhs, rhs, done):
                n = 0
                for a, b in ((0, 0), (0, 1), (1, 0)):
                    for k in range(KE):
                        last = pe.matmul(out, lhs(a, k), rhs(b, k), start=n == 0, stop=n == 3 * KE - 1)
                        n += 1
                last.then_inc(s[done], 1)

            x_of = lambda parity: lambda b, k: (xh, xl)[b][:, parity, k]

            def gate_up(n, parity, q, c):
                for g, out, done in ((0, GB(q), "g"), (1, UB(q), "u")):
                    three(out, lambda a, k: (w1h, w1l)[a][:, c, k, g], x_of(parity), done)
                if c < FM:
                    if c == 0:
                        pe.wait_ge(s["cT"], n + 1)
                    if not (first(n) and c == 0):
                        pe.wait_ge(s["p"], FC * n + c)
                    pe.matmul(CB, select[:, c], combT[:], start=True, stop=True).then_inc(s["cb"], 1)

            def down(n, q, c):
                pe.wait_ge(s["al"], FC * n + c + 1)
                if c == 0:
                    pe.wait_ge(s["oT"], KE * n)
                for m in range(KE):
                    for j, (w, t) in enumerate(((w2h, ah), (w2h, al), (w2l, ah))):
                        last = pe.matmul(OB(m), w[:, c, m * P:(m + 1) * P], t[:, q % 2], start=c == 0 and j == 0,
                                         stop=c == FC - 1 and j == 2)
                last.then_inc(s["s2"], 1)

            def transpose_rows(m, k):
                if k == 0:
                    pe.wait_ge(s["pxn"], m + 1)
                else:
                    pe.wait_ge(s["xl"], KE * m + 1)
                for b in range(B):
                    last = pe.transpose(X[:, b * P:(b + 1) * P], xp[:, b, k * P:(k + 1) * P], ident[:])
                last.then_inc(s["tx"], 1)

            def gate_logits(m, parity):
                pe.wait_ge(s["xl"], KE * m + KE)
                three(X, lambda a, k: (gt_h, gt_l)[a][:, k * NX:k * NX + P], x_of(parity), "lgT")

            def transpose_logits(m):
                pe.wait_ge(s["lgS"], m + 1)
                for b in range(B):
                    last = pe.transpose(X[:, b * P:(b + 1) * P], zT[:, b * P:(b + 1) * P], ident[:])
                last.then_inc(s["lgX"], 1)

            def transpose_weights(m):
                pe.wait_ge(s["comb3"], m + 1)
                xb = X.bitcast(BF16)
                for b in range(B):
                    last = pe.transpose(xb[0:3 * CR, b * P:(b + 1) * P], comb3[:, b].rearrange("p a e -> p (a e)"), ident_bf[:])
                last.then_inc(s["cx"], 1)

            def transpose_back(e, half):
                if half == 0:
                    pe.wait_ge(s["oT"], KE * (e + 1))
                else:
                    pe.wait_ge(s["x2"], 2 * e + 1)
                for j in range(2):
                    b = 2 * half + j
                    for m in range(KE):
                        last = pe.transpose(X[:, j * E + m * P:j * E + (m + 1) * P], backT[:, m, b * P:(b + 1) * P], ident[:])
                last.then_inc(s["back"], 1)

            for k in range(KE):
                transpose_rows(0, k)
            gate_logits(0, 0)
            transpose_logits(0)
            transpose_weights(0)
            pe.wait_ge(s["wl"], 2)
            pe.wait_ge(s["taps_a"], 2)
            gate_up(0, 0, 0, 0)

            def tile(n, parity, epilogue, prologue):
                for c in range(1, FC):
                    q = FC * parity + c
                    if first(n):
                        pe.wait_ge(s["wl"], 2 * c + 2)
                    gate_up(n, parity, q, c)
                    down(n, q - 1, c - 1)
                    if epilogue and c in (3, 5):
                        transpose_back(n - 1, (c - 3) // 2)
                    if prologue:
                        if c in (11, 13):
                            transpose_rows(n + 1, (c - 11) // 2)
                        if c == 15:
                            gate_logits(n + 1, 1 - parity)
                        if c == 18:
                            transpose_logits(n + 1)
                        if c == 23:
                            transpose_weights(n + 1)
                if prologue:
                    gate_up(n + 1, 1 - parity, FC * parity + FC, 0)
                down(n, FC * parity + FC - 1, FC - 1)

            tiles(pe, tile)
            for half in range(2):
                transpose_back(TT - 1, half)


CONV_LINKS = 2 * sum(B - m for m in range(1, LAGS)) + B
ROUTE_LINKS = 10


def selector():
    s = np.zeros((3, 32, FM * P), np.float32)
    f = np.arange(FM * P)
    s[:, f // IH, f] = 1.0
    return s.reshape(96, FM, P)


def rope_table():
    inv = (1.0 / np.float32(10000.0) ** (np.arange(0, D, 2, dtype=np.float32) / np.float32(D))).astype(np.float32)
    t = np.arange(N, dtype=np.float32)[:, None] * inv[None, :]
    c, s = np.cos(t), np.sin(t)
    both = np.stack([np.concatenate([c, c], 1), np.concatenate([-s, s], 1)])
    return np.ascontiguousarray(both.reshape(2, NT, P, D).transpose(2, 0, 1, 3)).astype(np.float32)


def kernel(L0_attn_a_x, L0_attn_a_w_qkv, L0_attn_a_w_out, L0_attn_a_ln_scale, L0_attn_a_ln_bias,
           L0_attn_b_delta, L0_attn_b_alpha, L0_attn_b_beta, L0_attn_b_gamma, L0_ffn_gate_w,
           L0_ffn_w1, L0_ffn_w2, L0_ffn_shared_w1, L0_ffn_shared_w2):
    import ml_dtypes
    import concourse.bacc as bacc
    from concourse.bass_utils import run_bass_kernel_spmd

    def blocks(w):
        return w.reshape(-1, P, w.shape[-1]).transpose(1, 0, 2)

    pad = FC * P - FM * P - SH
    w1 = np.asarray(L0_ffn_w1).reshape(NX, 2, IH, E)
    sw1 = np.asarray(L0_ffn_shared_w1).reshape(2, SH, E)
    both = [np.concatenate([w1[:, g].reshape(NX * IH, E), sw1[g], np.zeros((pad, E), np.float32)]) for g in range(2)]
    w1s = np.stack(both).reshape(2, FC, P, KE, P).transpose(4, 1, 3, 0, 2).reshape(P, FC, KE * 2 * P)
    w2s = np.concatenate([np.asarray(L0_ffn_w2).transpose(0, 2, 1).reshape(NX * IH, E),
                          np.asarray(L0_ffn_shared_w2).T, np.zeros((pad, E), np.float32)])
    gate = np.concatenate([*np.asarray(L0_ffn_gate_w).T.reshape(KE, P, NX), np.zeros((P, P - NX), np.float32)], 1)
    taps = np.stack([np.asarray(a).reshape(KE, P, 16) for a in
                     (L0_attn_b_delta, L0_attn_b_alpha, L0_attn_b_beta, L0_attn_b_gamma)])
    arrays = {
        "x": np.asarray(L0_attn_a_x).reshape(B, NT, P, E),
        "w_qkv": blocks(np.asarray(L0_attn_a_w_qkv)),
        "w_out": blocks(np.asarray(L0_attn_a_w_out)),
        "ln_affine": np.stack([np.asarray(L0_attn_a_ln_scale), np.asarray(L0_attn_a_ln_bias)]),
        "rope": rope_table(),
        "ident": np.eye(P, dtype=np.float32),
        "w1": w1s,
        "w2": blocks(w2s),
        "gate": gate,
        "taps": taps.transpose(2, 0, 1, 3).reshape(P, 4 * KE * 16),
        "select": selector().astype(ml_dtypes.bfloat16),
    }
    arrays = {n: np.ascontiguousarray(a) for n, a in arrays.items()}
    nc = bacc.Bacc("TRN2", target_bir_lowering=False, num_devices=1)
    t = {n: nc.dram_tensor(n, a.shape, mybir.dt.from_np(a.dtype), kind="ExternalInput").ap() for n, a in arrays.items()}
    x1 = nc.dram_tensor("x1", (B, NT, P, E), F32, kind="Internal").ap()
    x3 = nc.dram_tensor("x3", (B, NT, P, E), F32, kind="Internal").ap()
    out = nc.dram_tensor("out", (B, NT, P, E), F32, kind="ExternalOutput").ap()
    attention(nc, t["x"], t["w_qkv"], t["w_out"], t["ln_affine"], t["rope"], t["ident"], x1)
    feed_forward(nc, x1, t["w1"], t["w2"], t["gate"], t["taps"], t["select"], t["ident"], x3, out)
    r = run_bass_kernel_spmd(nc, [arrays], core_ids=[0])
    return r.results[0]["out"].reshape(B, N, E)
```

```python
from contextlib import ExitStack

import numpy as np

import concourse.bass as bass
from concourse import mybir

F32 = mybir.dt.float32
F32R = mybir.dt.float32r
BF16 = mybir.dt.bfloat16
ACT = mybir.ActivationFunctionType
ALU = mybir.AluOpType
AX = mybir.AxisListType

P = 128
B, N, E = 4, 1024, 256
H, D = 16, 16
KE = E // P
NT = N // P
G = 4
NG = NT // G
GT = G * P
H2 = 2 * H
PARTS = 6
KP = PARTS * D
EPS = 1e-5
ONE = 1

NX, TOPK, IH, SH = 16, 6, 176, 352
FM = NX * IH // P
FC = FM + -(-SH // P)
VW = 32
Q = 4
RA = 11
LAG = 8
LAGS = 4


def attention(nc, x, w_qkv, w_out, ln_affine, rope, ident_in, x1):
    ctx = ExitStack()
    with ctx:
        def sb(name, shape, dt=F32):
            return ctx.enter_context(nc.sbuf_tensor(name, shape, dt))

        def sem(name):
            return ctx.enter_context(nc.semaphore(name))

        psum = ctx.enter_context(nc.psum_tensor("attn_psum", [P, 8, 512], F32))

        ident = sb("a_ident", [P, P])
        ident_bf = sb("a_ident_bf", [P, P], BF16)
        rope_sb = sb("rope_sb", [P, 2, NT, D])
        affine = sb("affine", [P, 2, D])
        neg_half = sb("neg_half", [P, G])
        wq_h = sb("wq_h", [P, KE, 3 * E], F32R)
        wq_l = sb("wq_l", [P, KE, 3 * E], F32R)
        wo_h = sb("wo_h", [P, KE, E], F32R)
        wo_l = sb("wo_l", [P, KE, E], F32R)
        xa = sb("xa", [P, NT, E])
        xr = sb("xr", [P, NT, E])
        stats = sb("stats", [P, NT, 6])
        mv = sb("mv", [P, NT, 2])
        rstd = sb("rstd", [P, NT])
        pad = sb("pad", [P, 1])
        eps = sb("eps", [P, G])
        head_eps = sb("head_eps", [P, 1])
        xn = sb("xn", [P, NG, G, E])
        xh = sb("xh", [P, NG, KE, GT], F32R)
        xl = sb("xl", [P, NG, KE, GT], F32R)
        mean = sb("hmean", [P, 8, H2])
        var = sb("hvar", [P, 8, H2])
        hr = sb("hr", [P, 8, H2])
        parts = sb("parts", [P, 3, H2, PARTS, D], BF16)
        qt = sb("qt", [P, H, N], BF16)
        kt = sb("kt", [P, H, N], BF16)
        v = sb("v", [P, NT, H, VW])
        a = sb("a", [P, RA, 2, 512])
        wq_f = a[:].rearrange("p r h n -> p (r h n)")[:, 0:KE * 3 * E].rearrange("p (k n) -> p k n", k=KE)
        work, t2, sq = (a[:].rearrange("p r h n -> p (r h n)")[:, lo * 2 * GT:hi * 2 * GT]
                        .rearrange("p (i h d) -> p i h d", h=H2, d=D) for lo, hi in ((RA - 5, RA - 2), (RA - 2, RA - 1), (RA - 1, RA)))
        rec = sb("rec", [P, 2, G, Q])
        ot = sb("ot", [P, 2, 512])
        wo_f = ot[:].rearrange("p i n -> p (i n)")[:, 0:KE * E].rearrange("p (k n) -> p k n", k=KE)
        at_h, at_l = xh[:, 1], xl[:, 1]
        ao = parts[:].rearrange("p r h s d -> p (r h s d)")[:, 0:2 * NT * E].bitcast(F32).rearrange("p (i e) -> p i e", e=E)

        s_const = sem("s_const")
        s_ident = sem("s_ident")
        s_wq = sem("s_wq")
        s_made = sem("s_made")
        s_wsplit = sem("s_wsplit")
        s_wosplit = sem("s_wosplit")
        s_aTl = sem("s_aTl")
        s_xa = [sem(f"s_xa{g}") for g in range(NG)]
        s_xr = sem("s_xr")
        s_store = [sem(f"s_store{g}") for g in range(NG)]
        s_st = sem("s_st")
        s_stat = sem("s_stat")
        s_eps = sem("s_eps")
        s_rstd = sem("s_rstd")
        s_xn = sem("s_xn")
        s_xT = sem("s_xT")
        s_xh = sem("s_xh")
        s_xl = sem("s_xl")
        s_qkv = sem("s_qkv")
        s_v = sem("s_v")
        s_d1 = sem("s_d1")
        s_add = sem("s_add")
        s_m = sem("s_m")
        s_u = sem("s_u")
        s_sq = sem("s_sq")
        s_var = sem("s_var")
        s_sd = sem("s_sd")
        s_r = sem("s_r")
        s_w = sem("s_w")
        s_sc = sem("s_sc")
        s_wb = sem("s_wb")
        s_h1 = sem("s_h1")
        s_r1 = sem("s_r1")
        s_h2 = sem("s_h2")
        s_parts = sem("s_parts")
        s_tr = sem("s_tr")
        s_ev = sem("s_ev")
        s_evd = sem("s_evd")
        s_s = sem("s_s")
        s_q1 = sem("s_q1")
        s_a = sem("s_a")
        s_ad = sem("s_ad")
        s_ad1 = sem("s_ad1")
        s_passed = sem("s_passed")
        s_av = sem("s_av")
        s_rec = sem("s_rec")
        s_nrm = sem("s_nrm")
        s_ot = sem("s_ot")
        s_otT = sem("s_otT")
        s_aoT = sem("s_aoT")
        s_aT = sem("s_aT")
        s_y = sem("s_y")
        s_x1 = sem("s_x1")

        psT = lambda k: psum[:, k, :]
        psQK = lambda i: psum[:, 2 + i % 2, :].rearrange("p (h d) -> p h d", d=D)
        psV = psum[:, 4, 0:E]
        psTr = lambda k: psum[0:KP, 5 + k % 3, :].bitcast(BF16).rearrange("p (h t) -> p h t", h=8)
        S = lambda n: psum[:, 2 * (n % 3):2 * (n % 3) + 2, :]
        OT = lambda qc: psum[:, 6 + qc, :]

        LOWER = [(0, [(0, 0, range(0, 4))]),
                 (0, [(1, 0, range(1, 4)), (3, 384, range(3, 4))]),
                 (0, [(2, 0, range(2, 4))])]
        UPPER = [(1, [(j, 0, range(4, 8))]) for j in range(4)]
        CORNER = [(1, [(4, 0, range(4, 8))]),
                  (1, [(5, 0, range(5, 8)), (7, 384, range(7, 8))]),
                  (1, [(6, 0, range(6, 8))])]
        ORDER = [0, 1, 2, 3, 6, 8, 5, 9, 4, 7]
        UNITS = [(LOWER + UPPER + CORNER)[i] for i in ORDER]
        NU = len(UNITS)
        WORK = [(quad, u, half) for quad in range(H // Q) for u in range(NU) for half in range(2)]
        NB = len(WORK)
        width = lambda u: sum(len(o) * P for _, _, o in UNITS[u][1])
        diagonal = lambda u: UNITS[u][1][0][0] == UNITS[u][1][0][2][0]
        NDIAG = [sum(diagonal(u) for _, u, _ in WORK[:n]) for n in range(NB + 1)]
        LAST = [max(u for u in range(NU) if UNITS[u][0] == qc) for qc in range(2)]
        DONE = [n for n, (quad, u, half) in enumerate(WORK) if half and u in LAST]
        NQ = 2 * (H // Q)
        on_dve = lambda k: k // 4 >= 5 and k % 2 == 1
        N_DVE = [sum(on_dve(i) for i in range(k)) for k in range(4 * NT + 1)]
        N_ACT = [k - N_DVE[k] for k in range(4 * NT + 1)]
        STEPS = NT + 6

        AOT = lambda g, k: psum[:, 5 + g + k, :]
        Y = lambda g, c: psum[:, ((7, 5), (5, 6))[g][c], :]

        def batches(engine, prepare, heads, finish):
            prepare(0, None)
            with engine.Fori(0, B - 1) as b:
                heads(b, True)
                prepare(b + 1, b)
            heads(B - 1, False)
            for g in range(NG):
                finish(B - 1, g)

        block = ctx.enter_context(nc.Block())

        @block.sync
        def _(sp):
            for g in range(NG):
                sp.sem_inc(s_store[g], ONE)

            def first_rows(g):
                sp.dma_start(xa[:, G * g:G * g + G, :], x[0, G * g:G * g + G, :, :].rearrange("t p e -> p t e")).then_inc(s_xa[g], 16)

            first_rows(0)
            sp.dma_start(wq_f, w_qkv).then_inc(s_wq, 16)
            sp.dma_start(ident[:], ident_in).then_inc(s_ident, 16)
            first_rows(1)
            sp.dma_start(rope_sb[:], rope).then_inc(s_const, 16)
            sp.dma_start(affine[:], ln_affine.partition_broadcast(P)).then_inc(s_const, 16)
            sp.dma_start(wo_f, w_out).then_inc(s_const, 16)

            def load_rows(b):
                for g in range(NG):
                    sp.dma_start(xa[:, G * g:G * g + G, :],
                                 x[bass.ds(b, 1), G * g:G * g + G, :, :].rearrange("o t p e -> p (o t) e")
                                 ).then_inc(s_xa[g], 16)

            def batch(b, more):
                if more:
                    sp.wait_ge(s_xn, ONE + NT * b + NT)
                    load_rows(b + 1)
                for g in range(NG):
                    sp.wait_ge(s_store[g], ONE + 16 * b)
                sp.dma_start(xr[:], x[bass.ds(b, 1), :, :, :].rearrange("o t p e -> p (o t) e")).then_inc(s_xr, 16)
                for g in range(NG):
                    sp.wait_ge(s_x1, ONE + 2 * NG * b + 2 * g + 2)
                    sp.dma_start(x1[bass.ds(b, 1), G * g:G * g + G, :, :].rearrange("o t p e -> p (o t) e"),
                                 xr[:, G * g:G * g + G, :]).then_inc(s_store[g], 16)

            with sp.Fori(0, B - 1) as b:
                batch(b, True)
            batch(B - 1, False)
            for g in range(NG):
                sp.wait_ge(s_store[g], ONE + 16 * B)

        @block.gpsimd
        def _(pool):
            pool.memset(v[:, :, :, D + 1:], 0.0)
            pool.memset(v[:, :, :, D:D + 1], 1.0).then_inc(s_made, 1)
            pool.memset(neg_half[:], -0.5).then_inc(s_made, 1)
            pool.memset(eps[:], EPS).then_inc(s_made, 1)
            pool.memset(head_eps[:], EPS).then_inc(s_made, 1)
            pool.wait_ge(s_made, 4)

            def token_rstd(b, g):
                n = NG * b + g
                pool.wait_ge(s_stat, n + 1)
                r = rstd[:, G * g:G * g + G]
                pool.tensor_tensor(r, mv[:, G * g:G * g + G, 1], eps[:], ALU.add).then_inc(s_eps, 1)
                pool.wait_ge(s_eps, n + 1)
                pool.tensor_tensor(r, r, neg_half[:, 0:G], ALU.pow).then_inc(s_rstd, 1)

            def prepare(b, out):
                for s in range(STEPS):
                    if 0 <= (i := s - 4) < NT:
                        w = work[:, i % 6]
                        pool.wait_ge(s_h1, NT * b + i + 1)
                        pool.tensor_tensor(w, w, parts[:, i % 3, :, 0, :], ALU.subtract).then_inc(s_r1, 1)
                    if 0 <= (i := s - 3) < NT:
                        pool.wait_ge(s_w, NT * b + i + 1)
                        w = work[:, i % 6]
                        pool.tensor_tensor(w, w, affine[:, 0:1, :].to_broadcast([P, H2, D]), ALU.mult).then_inc(s_sc, 1)
                        pool.wait_ge(s_sc, NT * b + i + 1)
                        pool.tensor_tensor(w, w, affine[:, 1:2, :].to_broadcast([P, H2, D]), ALU.add).then_inc(s_wb, 1)
                    if (i := s) < NT:
                        pool.wait_ge(s_d1, NT * b + i + 1)
                        w = work[:, i % 6]
                        pool.tensor_tensor(w, w, t2[:, i % 2], ALU.add).then_inc(s_add, 1)

            def heads(b, more):
                if more:
                    for g in range(NG):
                        token_rstd(b + 1, g)
                for n, (quad, u, half) in enumerate(WORK):
                    if not diagonal(u):
                        continue
                    pool.wait_ge(s_q1, NB * b + n + 1)
                    two = len(UNITS[u][1])
                    d = a[:, n % RA].rearrange("p h (o q) -> p h o q", q=P)[:, :, 0:3 * two - 2:3, :]
                    pool.tensor_tensor(d, d, d, ALU.mult).then_inc(s_ad1, 1)
                    pool.wait_ge(s_ad1, NDIAG[NB] * b + NDIAG[n] + 1)
                    pool.sem_inc(s_passed, 1)
                    for k in range(two):
                        last = pool.affine_select(out=d[:, :, k], in_=d[:, :, k], compare_op=ALU.is_ge, fill=0.0,
                                                  base=0, pattern=[[0, 2], [1, P]], channel_multiplier=-1)
                    last.then_inc(s_ad, 1)

            for g in range(NG):
                token_rstd(0, g)
            pool.wait_ge(s_const, 48)
            batches(pool, prepare, heads, lambda b, g: None)

        @block.scalar
        def _(act):
            act.sem_inc(s_v, ONE)
            act.sem_inc(s_ev, ONE)
            act.wait_ge(s_ident, 16)
            act.activation(ident_bf[:], ident[:], ACT.Copy).then_inc(s_wsplit, 1)
            act.wait_ge(s_wq, 16)
            act.activation(wq_h[:], wq_f, ACT.Copy).then_inc(s_wsplit, 1)
            act.wait_ge(s_made, 4)
            act.wait_ge(s_const, 48)
            act.activation(wo_h[:], wo_f, ACT.Copy).then_inc(s_wosplit, 1)
            def keep_output(b, m):
                act.wait_ge(s_av, ONE + NB // 2 * b + (DONE[m] + 1) // 2)
                act.activation(ot[:, m % 2, :], OT(m % 2), ACT.Copy).then_inc(s_ot, 1)

            def transposed_out(b, g):
                if g:
                    act.wait_ge(s_y, 4 * b + 2)
                for k in range(KE):
                    act.wait_ge(s_aoT, 4 * b + 2 * g + k + 1)
                    act.activation(at_h[:, k, :], AOT(g, k), ACT.Copy).then_inc(s_aT, 1)

            def finish(b, g):
                if g == 0:
                    keep_output(b, NQ - 1)
                transposed_out(b, g)

            def high_rows(b, g, out):
                if out is not None:
                    act.wait_ge(s_y, 4 * out + 4)
                for k in range(KE):
                    act.wait_ge(s_xT, 4 * b + 2 * g + k + 1)
                    act.activation(xh[:, g, k, :], psT(k), ACT.Copy).then_inc(s_xh, 1)

            def prepare(b, out):
                for s in range(STEPS):
                    if s == 0:
                        high_rows(b, 0, None)
                    if out is not None and s == 0:
                        transposed_out(out, 0)
                    if out is not None and s == 0:
                        keep_output(out, NQ - 1)
                    if (i := s) < NT:
                        act.wait_ge(s_qkv, NT * b + i + 1)
                        act.activation(v[:, i, :, 0:D], psV.rearrange("p (h d) -> p h d", d=D), ACT.Copy).then_inc(s_v, 1)
                    if out is not None and s == 2:
                        transposed_out(out, 1)
                    if s == G - 1:
                        high_rows(b, 1, out)
                    if 0 <= (i := s - 6) < NT:
                        for c in range(4):
                            if on_dve(4 * i + c):
                                continue
                            act.wait_ge(s_tr, 4 * NT * b + 4 * i + c + 1)
                            to = (qt, kt)[c // 2]
                            act.activation(to[0:KP, 8 * (c % 2):8 * (c % 2) + 8, i * P:(i + 1) * P], psTr(4 * i + c),
                                           ACT.Copy).then_inc(s_ev, 1)
                    if 0 <= (i := s - 2) < NT:
                        act.wait_ge(s_var, NT * b + i + 1)
                        act.activation(hr[:, i], var[:, i], ACT.Sqrt, bias=head_eps[:], scale=1.0 / D).then_inc(s_sd, 1)
                    if 0 <= (i := s - 4) < NT:
                        act.wait_ge(s_r1, NT * b + i + 1)
                        act.activation(parts[:, i % 3, :, 1, :], work[:, i % 6], ACT.Copy).then_inc(s_h2, 1)
                    if 0 <= (i := s - 3) < NT:
                        act.wait_ge(s_wb, NT * b + i + 1)
                        act.activation(parts[:, i % 3, :, 0, :], work[:, i % 6], ACT.Copy).then_inc(s_h1, 1)
                    if 0 <= (i := s - 1) < NT:
                        act.wait_ge(s_u, NT * b + i + 1)
                        if i >= 2:
                            act.wait_ge(s_var, NT * b + i - 1)
                        act.activation(sq[:, i % 2], work[:, i % 6], ACT.Square).then_inc(s_sq, 1)

            def heads(b, more):
                m = 0
                for n, (quad, u, half) in enumerate(WORK):
                    act.wait_ge(s_s, NB * b + n + 1)
                    act.wait_ge(s_av, ONE + NB // 2 * b + max(0, (n - RA) // 2 + 1))
                    w = width(u)
                    act.activation(a[:, n % RA, :, 0:w], S(n)[:, :, 0:w], ACT.Square).then_inc(s_q1, 1)
                    if n - LAG in DONE:
                        keep_output(b, m)
                        m += 1

            batches(act, prepare, heads, finish)

        @block.vector
        def _(dve):
            for free in (s_xn, s_xl, s_nrm, s_x1, s_evd):
                dve.sem_inc(free, ONE)

            def normalise(b, g):
                n = NG * b + g
                dve.wait_ge(s_xa[g], 16 * b + 16)
                for t in range(G * g, G * g + G):
                    dve.bn_stats(stats[:, t, :], xa[:, t, :]).then_inc(s_st, 1)
                dve.wait_ge(s_st, NT * b + G * g + G)
                dve.memset(pad[:], 0.0)
                for t in range(G * g, G * g + G):
                    last = dve.bn_aggr(mv[:, t, :], stats[:, t, :])
                last.then_inc(s_stat, 1)

            def normalise2(b, g):
                dve.wait_ge(s_rstd, NG * b + g + 1)
                for t in range(G):
                    i = G * g + t
                    dve.tensor_scalar(xn[:, g, t, :], xa[:, i, :], mv[:, i, 0:1], rstd[:, i:i + 1],
                                      ALU.subtract, ALU.mult).then_inc(s_xn, 1)

            def norm(b, m):
                quad, qc = m // 2, m % 2
                dve.wait_ge(s_otT, NQ * b + m + 1)
                o = OT(qc).rearrange("p (i h d) -> p i h d", h=Q, d=VW)
                r = rec[:, qc]
                dve.reciprocal(r, o[:, :, :, D]).then_inc(s_rec, 1)
                dve.wait_ge(s_rec, NQ * b + m + 1)
                to = ao[:, G * qc:G * qc + G, Q * D * quad:Q * D * quad + Q * D].rearrange("p i (h d) -> p i h d", d=D)
                dve.tensor_tensor(to, o[:, :, :, 0:D], r.unsqueeze(3).to_broadcast([P, G, Q, D]),
                                  ALU.mult).then_inc(s_nrm, 1)

            def finish(b, g):
                if g == 0:
                    dve.wait_ge(s_xr, 16 * b + 16)
                for c in range(2):
                    dve.wait_ge(s_y, 4 * b + 2 * g + c + 1)
                    t = xr[:, G * g + 2 * c:G * g + 2 * c + 2, :]
                    dve.tensor_tensor(t, t, Y(g, c).rearrange("p (t e) -> p t e", e=E), ALU.add).then_inc(s_x1, 1)

            def low_out(b, g):
                for k in range(KE):
                    dve.wait_ge(s_aT, 4 * b + 2 * g + k + 1)
                    dve.tensor_tensor(at_l[:, k, :], AOT(g, k), at_h[:, k, :].bitcast(F32), ALU.subtract).then_inc(s_aTl, 1)

            def last_norm_and_finish(b, g):
                if g == 0:
                    norm(b, NQ - 1)
                low_out(b, g)
                finish(b, g)

            def low_rows(b, g):
                for k in range(KE):
                    dve.wait_ge(s_xh, 4 * b + 2 * g + k + 1)
                    dve.tensor_tensor(xl[:, g, k, :], psT(k), xh[:, g, k, :].bitcast(F32), ALU.subtract).then_inc(s_xl, 1)

            def prepare(b, out):
                for s in range(STEPS):
                    if s == 0:
                        low_rows(b, 0)
                    if 0 <= (i := s - 3) < NT:
                        w = work[:, i % 6]
                        dve.wait_ge(s_sd, NT * b + i + 1)
                        dve.reciprocal(hr[:, i], hr[:, i]).then_inc(s_r, 1)
                        dve.wait_ge(s_r, NT * b + i + 1)
                        dve.tensor_tensor(w, w, hr[:, i].unsqueeze(2).to_broadcast([P, H2, D]), ALU.mult).then_inc(s_w, 1)
                    if out is not None and s == 0:
                        low_out(out, 0)
                    if (i := s) < NT:
                        dve.wait_ge(s_qkv, NT * b + i + 1)
                        qk = psQK(i)
                        w, t = work[:, i % 6], t2[:, i % 2]
                        hd = D // 2
                        dve.tensor_tensor(w, qk, rope_sb[:, 0, i:i + 1, :].to_broadcast([P, H2, D]), ALU.mult)
                        dve.tensor_tensor(t[:, :, 0:hd], qk[:, :, hd:D],
                                          rope_sb[:, 1, i:i + 1, 0:hd].to_broadcast([P, H2, hd]), ALU.mult)
                        dve.tensor_tensor(t[:, :, hd:D], qk[:, :, 0:hd],
                                          rope_sb[:, 1, i:i + 1, hd:D].to_broadcast([P, H2, hd]), ALU.mult
                                          ).then_inc(s_d1, 1)
                    if out is not None and s == 2:
                        low_out(out, 1)
                    if s == G - 1:
                        low_rows(b, 1)
                    if 0 <= (i := s - 2) < NT:
                        dve.wait_ge(s_sq, NT * b + i + 1)
                        dve.reduce_sum(var[:, i], sq[:, i % 2], AX.X).then_inc(s_var, 1)
                    if 0 <= (i := s - 5) < NT:
                        w, q, k = work[:, i % 6], parts[:, i % 3, 0:H], parts[:, i % 3, H:H2]
                        dve.wait_ge(s_h2, NT * b + i + 1)
                        dve.tensor_tensor(q[:, :, 5, :], w[:, 0:H], q[:, :, 1, :], ALU.subtract)
                        dve.tensor_tensor(k[:, :, 4, :], w[:, H:H2], k[:, :, 1, :], ALU.subtract)
                        dve.tensor_copy(q[:, :, 2, :], q[:, :, 0, :])
                        dve.tensor_copy(q[:, :, 4, :], q[:, :, 0, :])
                        dve.tensor_copy(q[:, :, 3, :], q[:, :, 1, :])
                        dve.tensor_copy(k[:, :, 3, :], k[:, :, 0, :])
                        dve.tensor_copy(k[:, :, 5, :], k[:, :, 0, :])
                        dve.tensor_copy(k[:, :, 2, :], k[:, :, 1, :]).then_inc(s_parts, 1)
                    if 0 <= (i := s - 6) < NT:
                        for c in range(4):
                            if on_dve(4 * i + c):
                                dve.wait_ge(s_tr, 4 * NT * b + 4 * i + c + 1)
                                to = (qt, kt)[c // 2]
                                dve.tensor_copy(to[0:KP, 8 * (c % 2):8 * (c % 2) + 8, i * P:(i + 1) * P], psTr(4 * i + c)).then_inc(s_evd, 1)
                    if 0 <= (i := s - 1) < NT:
                        w = work[:, i % 6]
                        dve.wait_ge(s_add, NT * b + i + 1)
                        dve.reduce_sum(mean[:, i], w, AX.X).then_inc(s_m, 1)
                        dve.wait_ge(s_m, NT * b + i + 1)
                        dve.scalar_tensor_tensor(out=w, in0=mean[:, i].unsqueeze(2).to_broadcast([P, H2, D]),
                                                 scalar=-1.0 / D, in1=w, op0=ALU.mult, op1=ALU.add).then_inc(s_u, 1)
                    if out is not None and s in (1, 3):
                        finish(out, s // 2)
                    if out is not None and s == 0:
                        norm(out, NQ - 1)

            def heads(b, more):
                if more:
                    for g in range(NG):
                        normalise(b + 1, g)
                    for g in range(NG):
                        normalise2(b + 1, g)
                m = 0
                for n, (quad, u, half) in enumerate(WORK):
                    lo = P if diagonal(u) else 0
                    hi = UNITS[u][1][1][1] if len(UNITS[u][1]) > 1 else width(u)
                    dve.wait_ge(s_q1, NB * b + n + 1)
                    t = a[:, n % RA, :, lo:hi]
                    dve.tensor_tensor(t, t, t, ALU.mult).then_inc(s_a, 1)
                    if n - LAG - 3 in DONE:
                        norm(b, m)
                        m += 1

            normalise(0, 0)
            normalise(0, 1)
            normalise2(0, 0)
            dve.wait_ge(s_wsplit, 2)
            dve.tensor_tensor(wq_l[:], wq_f, wq_h[:].bitcast(F32), ALU.subtract).then_inc(s_wsplit, 1)
            normalise2(0, 1)
            dve.wait_ge(s_const, 48)
            dve.wait_ge(s_wosplit, 1)
            dve.tensor_tensor(wo_l[:], wo_f, wo_h[:].bitcast(F32), ALU.subtract).then_inc(s_wosplit, 1)
            batches(dve, prepare, heads, last_norm_and_finish)

        @block.tensor
        def _(pe):
            pe.sem_inc(s_av, ONE)
            pe.wait_ge(s_ident, 16)

            def transpose_rows(b, g):
                pe.wait_ge(s_xn, ONE + NT * b + G * g + G)
                pe.wait_ge(s_xl, ONE + 4 * b + 2 * g)
                for k in range(KE):
                    for t in range(G):
                        last = pe.transpose(psT(k)[:, t * P:(t + 1) * P], xn[:, g, t, k * P:(k + 1) * P], ident[:])
                    last.then_inc(s_xT, 1)

            def project(b, i, g, t):
                for out, lo, hi in ((psum[:, 2 + i % 2, :], 0, 2 * E), (psV, 2 * E, 3 * E)):
                    n = 0
                    if out is psV:
                        pe.wait_ge(s_v, ONE + NT * b + i)
                    for xs, ws in ((xh, wq_h), (xh, wq_l), (xl, wq_h)):
                        for k in range(KE):
                            last = pe.matmul(out, xs[:, g, k, t * P:(t + 1) * P], ws[:, k, lo:hi],
                                             start=n == 0, stop=n == 3 * KE - 1)
                            n += 1
                last.then_inc(s_qkv, 1)

            def outputs(b, m):
                pe.wait_ge(s_ot, NQ * b + m + 1)
                for i in range(G):
                    last = pe.transpose(OT(m % 2)[:, i * P:(i + 1) * P], ot[:, m % 2, i * P:(i + 1) * P], ident[:])
                last.then_inc(s_otT, 1)

            def transpose_out(b, g):
                pe.wait_ge(s_nrm, ONE + NQ * b + NQ - 1 + g)
                for k in range(KE):
                    if g:
                        pe.wait_ge(s_x1, ONE + 4 * b + 2)
                    for t in range(G):
                        last = pe.transpose(AOT(g, k)[:, t * P:(t + 1) * P], ao[:, G * g + t, k * P:(k + 1) * P], ident[:])
                    last.then_inc(s_aoT, 1)

            def project_out(b, g):
                if g == 0:
                    pe.wait_ge(s_nrm, ONE + NQ * b + NQ)
                pe.wait_ge(s_aTl, 4 * b + 2 * g + 2)
                for t in range(G):
                    n = 0
                    for rows, ws in ((at_h, wo_h), (at_h, wo_l), (at_l, wo_h)):
                        for k in range(KE):
                            last = pe.matmul(Y(g, t // 2)[:, (t % 2) * E:(t % 2) * E + E], rows[:, k, t * P:(t + 1) * P],
                                             ws[:, k, :], start=n == 0, stop=n == 3 * KE - 1)
                            n += 1
                    if t % 2:
                        last.then_inc(s_y, 1)

            def finish(b, g):
                transpose_out(b, g)
                if g == 0:
                    outputs(b, NQ - 1)
                project_out(b, g)

            def prepare(b, out):
                for s in range(STEPS):
                    if s == 0:
                        transpose_rows(b, 0)
                        if out is not None:
                            transpose_out(out, 0)
                            outputs(out, NQ - 1)
                    if s % G == 0 and s < NT:
                        pe.wait_ge(s_xl, ONE + 4 * b + 2 * (s // G) + 2)
                    if (i := s) < NT:
                        if i >= 2:
                            pe.wait_ge(s_d1, NT * b + i - 1)
                        if out is None and i == 0:
                            pe.wait_ge(s_wsplit, 3)
                            pe.wait_ge(s_const, 48)
                        project(b, i, i // G, i % G)
                    if s == G - 1:
                        transpose_rows(b, 1)
                    if out is not None and s == 2:
                        transpose_out(out, 1)
                    if out is not None and s in (1, 3):
                        project_out(out, s // 2)
                    if 0 <= (i := s - 6) < NT:
                        pe.wait_ge(s_parts, NT * b + i + 1)
                        if i == 0:
                            pe.wait_ge(s_x1, ONE + 4 * b)
                        for c in range(4):
                            k = 4 * i + c
                            if k >= 3:
                                if on_dve(k - 3):
                                    pe.wait_ge(s_evd, ONE + N_DVE[-1] * b + N_DVE[k - 2])
                                else:
                                    pe.wait_ge(s_ev, ONE + N_ACT[-1] * b + N_ACT[k - 2])
                            for h in range(8):
                                last = pe.transpose(psTr(4 * i + c)[:, h, :], parts[:, i % 3, 8 * c + h], ident_bf[:])
                            last.then_inc(s_tr, 1)
            def heads(b, more):
                pe.wait_ge(s_ev, ONE + N_ACT[-1] * (b + 1))
                pe.wait_ge(s_evd, ONE + N_DVE[-1] * (b + 1))
                pe.wait_ge(s_v, ONE + NT * b + NT)

                def scores(n):
                    quad, u, half = WORK[n]
                    if n >= 3:
                        pe.wait_ge(s_q1, NB * b + n - 2)
                    for hh in range(2):
                        h = Q * quad + 2 * half + hh
                        for j, col, tiles in UNITS[u][1]:
                            w = len(tiles) * P
                            last = pe.matmul(S(n)[:, hh, col:col + w], kt[0:KP, h, j * P:(j + 1) * P],
                                             qt[0:KP, h, tiles[0] * P:tiles[0] * P + w], start=True, stop=True)
                    last.then_inc(s_s, 1)

                def values(n):
                    quad, u, _ = WORK[n]
                    qc = UNITS[u][0]
                    pe.wait_ge(s_a, NB * b + n + 1)
                    if diagonal(u):
                        pe.wait_ge(s_ad, NDIAG[NB] * b + NDIAG[n + 1])
                    if UNITS[u][1][0][0] == 0:
                        pe.wait_ge(s_nrm, ONE + NQ * b + max(0, 2 * quad + qc - 1))
                    for j, col, tiles in UNITS[u][1]:
                        w = len(tiles) * P
                        at_ = (tiles[0] - 4 * qc) * P
                        for hh in range(Q):
                            last = pe.matmul(OT(qc)[VW * hh:VW * hh + VW, at_:at_ + w], v[:, j, Q * quad + hh, :],
                                             a[:, (n - 1 + hh // 2) % RA, hh % 2, col:col + w],
                                             start=j == 0, stop=j == 4 * qc + 3, skip_group_check=True)
                    last.then_inc(s_av, 1)

                m = 0
                for n in range(NB + LAG):
                    if n < NB:
                        scores(n)
                    if n > LAG and (n - LAG) % 2:
                        values(n - LAG)
                    if n - LAG - 3 in DONE:
                        outputs(b, m)
                        m += 1

            batches(pe, prepare, heads, finish)


def feed_forward(nc, x1, w1, w2, gate, taps_in, ident_in, weights_t, x3, out):
    ctx = ExitStack()
    with ctx:
        def sb(name, shape, dt=F32):
            return ctx.enter_context(nc.sbuf_tensor(name, shape, dt))

        def sem(name):
            return ctx.enter_context(nc.semaphore(name))

        psum = ctx.enter_context(nc.psum_tensor("ffn_psum", [P, 8, 512], F32))
        TT = 2 * NT
        TOK = B * P
        RING = 3
        PIECES = [[(max(0, e * IH - c * P), min(P, (e + 1) * IH - c * P), e) for e in range(c * P // IH, ((c + 1) * P - 1) // IH + 1)]
                  for c in range(FM)]
        loads_to = lambda c: sum(len(PIECES[i]) for i in range(c % RING, c + 1, RING))
        LOADS = [loads_to(max(range(r, FM, RING))) for r in range(RING)]

        w1h = sb("w1h", [P, FC, KE, 2, P], F32R)
        w1l = sb("w1l", [P, FC, KE, 2, P], F32R)
        w2h = sb("w2h", [P, FC, E], F32R)
        w2l = sb("w2l", [P, FC, E], F32R)
        GW = KE * NX + P - NX
        gt_h = sb("gt_h", [P, GW], F32R)
        gt_l = sb("gt_l", [P, GW], F32R)
        ident = sb("f_ident", [P, P])
        taps = sb("taps_sb", [P, LAGS, E])
        xp = sb("xp", [P, B, E])
        xe = sb("xe", [P, B, E])
        back = sb("back", [P, B * E])
        z = sb("z", [P, B, E])
        tmp = sb("tmp", [P, E])
        xh = sb("f_xh", [P, 2, KE, TOK], F32R)
        xl = sb("f_xl", [P, 2, KE, TOK], F32R)
        pr = sb("pr", [P, TOK])
        ah = sb("ah", [P, 2, TOK], F32R)
        al = sb("al", [P, 2, TOK], F32R)
        cbs = sb("cbs", [P, RING, TOK])
        stats = sb("f_stats", [P, 2, B, 6])
        mv = sb("f_mv", [P, 2, B, 2])
        rstd = sb("f_rstd", [P, 2, B])
        eps = sb("f_eps", [P, B])
        neg_half = sb("f_half", [P, B])
        pad = sb("f_pad", [P, 1])
        zero = sb("f_zero", [P, 1])
        mx = sb("mx", [P, B])
        rest = sb("rest", [P, B, NX + 2])
        lg = rest[:, :, 0:NX]
        prob = sb("prob", [P, B, NX + 2])
        top = sb("top", [P, B, 8])
        comb = prob[:, :, 0:NX]
        kcol = sb("kcol", [P, LAGS, KE])
        taps_raw = z[:].rearrange("p a b -> p (a b)")[:, TOK:TOK + 4 * KE * 16]
        tw = taps_raw.rearrange("p (s h n) -> p s h n", s=4, h=KE)

        names = """const made wh wl gsplit taps_a taps_v taps_d taps_in taps_p pst peps prs pxn tx xh xl
                   lgT lgS lgX sm ex comb cx cT cw g u silu p1 p ah al s2 oT back x2 cst ceps crs cy plink clink mx
                   conv_link csilu x3 xp xe store link""".split()
        s = {n: sem("f_" + n) for n in names}
        s_wst = [sem("f_wst0"), sem("f_wst1")]
        s_cb = [sem(f"f_cb{r}") for r in range(RING)]

        GB = lambda q: psum[:, 2 * (q % 2), :]
        UB = lambda q: psum[:, 2 * (q % 2) + 1, :]
        OB = lambda m: psum[:, 5 + m, :]
        X = psum[:, 7, :]
        stage1 = xe[:].rearrange("p b e -> p (b e)").rearrange("p (i n) -> p i n", i=2)
        stage2 = back[:].rearrange("p (i n) -> p i n", i=4)
        backT = back[:].rearrange("p (m n) -> p m n", m=KE)
        backY = back[:].rearrange("p (b e) -> p b e", e=E)
        zT = z[:].rearrange("p b e -> p (b e)")[:, 0:TOK]
        combT = zT[0:NX]

        def tiles(engine, tile):
            tile(0, 0, None, True)
            tile(1, 1, "conv", True)
            with engine.Fori(1, NT // 2) as i:
                tile(2 * i, 0, "conv", True)
                tile(2 * i + 1, 1, "conv", True)
            tile(NT, 0, "conv", True)
            tile(NT + 1, 1, "plain", True)
            with engine.Fori(NT // 2 + 1, NT - 1) as i:
                tile(2 * i, 0, "plain", True)
                tile(2 * i + 1, 1, "plain", True)
            tile(TT - 2, 0, "plain", True)
            tile(TT - 1, 1, "plain", False)

        first = lambda n: isinstance(n, int) and n == 0

        block = ctx.enter_context(nc.Block())

        @block.sync
        def _(sp):
            def rows(dram, t):
                return dram[:, bass.ds(t, 1), :, :].rearrange("b o p e -> p (b o) e")

            def load(to, n, second, name):
                sp.dma_start(to[:], rows(x3, n - NT) if second else rows(x1, n)).then_inc(s[name], 16)

            sp.sem_inc(s["store"], ONE)
            load(xp, 0, False, "xp")
            sp.dma_start(ident[:], ident_in).then_inc(s["const"], 16)
            sp.dma_start(pr[:, 0:GW], gate).then_inc(s["const"], 16)
            sp.dma_start(taps_raw, taps_in).then_inc(s["taps_in"], 16)
            def stage(c):
                if c >= 2:
                    sp.wait_ge(s["wl"], 2 * (c - 1))
                sp.dma_start(stage1[:, c % 2, :], w1[:, c]).then_inc(s_wst[c % 2], 16)
                sp.dma_start(stage2[:, c % 2, :], w2[:, c]).then_inc(s_wst[c % 2], 16)

            def spread(n, c):
                if c >= RING:
                    sp.wait_ge(s["p"], FC * n + c - RING + 1)
                for lo, hi, e in PIECES[c]:
                    sp.dma_start(cbs[lo:hi, c % RING, :], weights_t[e].partition_broadcast(hi - lo)).then_inc(s_cb[c % RING], 16)

            def weights_out(n):
                sp.wait_ge(s["cT"], n + 1)
                sp.dma_start(weights_t, combT).then_inc(s["cw"], 16)
                sp.wait_ge(s["cw"], 16 * n + 16)
                for c in range(RING):
                    spread(n, c)

            for c in range(4):
                stage(c)
            weights_out(0)
            for c in range(RING, FC):
                if c < FM:
                    spread(0, c)
                if c + 1 < FC:
                    stage(c + 1)
                if c == 4:
                    sp.wait_ge(s["tx"], KE)
                    load(xp, 1, False, "xp")
            sp.wait_ge(s["wl"], 2 * FC)
            weights_out(1)

            def turn(n, loads_second, residual_second, store_to, prologue):
                sp.wait_ge(s["store"], ONE + 16 * (n - 1))
                load(xe, n - 1, residual_second, "xe")
                if prologue:
                    sp.wait_ge(s["tx"], KE * (n + 1))
                    load(xp, n + 1, loads_second, "xp")
                last = isinstance(n, int) and n == TT
                if not last:
                    for c in range(RING, FM - 1):
                        spread(n, c)
                if store_to is x3:
                    sp.wait_ge(s["x3"], n)
                    sp.dma_start(rows(x3, n - 1), xe[:]).then_inc(s["store"], 16)
                else:
                    sp.wait_ge(s["x2"], 2 * n)
                    sp.dma_start(rows(out, n - 1 - NT), xe[:]).then_inc(s["store"], 16)
                if not last:
                    spread(n, FM - 1)
                if prologue:
                    weights_out(n + 1)

            with sp.Fori(1, NT - 1) as n:
                turn(n, False, False, x3, True)
            turn(NT - 1, True, False, x3, True)
            turn(NT, True, False, x3, True)
            with sp.Fori(NT + 1, TT - 1) as n:
                turn(n, True, True, out, True)
            turn(TT - 1, True, True, out, False)
            turn(TT, True, True, out, False)
            sp.wait_ge(s["store"], ONE + 16 * TT)

        @block.gpsimd
        def _(pool):
            pool.memset(eps[:], EPS).then_inc(s["made"], 1)
            pool.memset(neg_half[:], -0.5).then_inc(s["made"], 1)
            pool.memset(prob[:, :, NX:NX + 1], -1.0).then_inc(s["made"], 1)
            pool.memset(prob[:, :, NX + 1:], -2.0).then_inc(s["made"], 1)
            pool.memset(tmp[:, 0:P], 1.0).then_inc(s["made"], 1)
            pool.memset(zero[:], 0.0).then_inc(s["made"], 1)
            pool.wait_ge(s["made"], 6)

            def rstd_of(which, ready, added, done, m):
                pool.wait_ge(s[ready], m + 1)
                r = rstd[:, which]
                pool.tensor_tensor(r, mv[:, which, :, 1], eps[:], ALU.add).then_inc(s[added], 1)
                pool.wait_ge(s[added], m + 1)
                pool.tensor_tensor(r, r, neg_half[:], ALU.pow).then_inc(s[done], 1)

            def convolve(e):
                pool.wait_ge(s["cy"], e + 1)
                if first(e):
                    pool.wait_ge(s["taps_a"], 3)
                links = e * CONV_LINKS
                for l in range(B):
                    pool.tensor_tensor(z[:, l], backY[:, l], taps[:, 0], ALU.mult).then_inc(s["conv_link"], 1)
                    links = links + 1
                for m in range(1, LAGS):
                    for l in range(m, B):
                        pool.wait_ge(s["conv_link"], links)
                        pool.tensor_tensor(tmp[:], backY[:, l - m], taps[:, m], ALU.mult).then_inc(s["conv_link"], 1)
                        links = links + 1
                        pool.wait_ge(s["conv_link"], links)
                        last = pool.tensor_tensor(z[:, l], z[:, l], tmp[:], ALU.add)
                        last.then_inc(s["conv_link"], 1)
                        links = links + 1

            rstd_of(0, "pst", "peps", "prs", 0)

            def tile(n, parity, epilogue, prologue):
                if epilogue == "conv":
                    rstd_of(1, "cst", "ceps", "crs", n - 1)
                if prologue:
                    rstd_of(0, "pst", "peps", "prs", n + 1)
                if epilogue == "conv":
                    convolve(n - 1)

            tiles(pool, tile)

        @block.scalar
        def _(act):
            act.wait_ge(s["const"], 32)
            act.wait_ge(s["made"], 6)
            act.activation(gt_h[:], pr[:, 0:GW], ACT.Copy).then_inc(s["gsplit"], 1)

            def split(c):
                act.wait_ge(s_wst[c % 2], 32 * (c // 2) + 32)
                act.activation(w1h[:, c].rearrange("p k g f -> p (k g f)"), stage1[:, c % 2, :], ACT.Copy).then_inc(s["wh"], 1)
                act.activation(w2h[:, c], stage2[:, c % 2, :], ACT.Copy).then_inc(s["wh"], 1)

            def high(m, parity, k):
                act.wait_ge(s["tx"], KE * m + k + 1)
                act.activation(xh[:, parity, k], X, ACT.Copy).then_inc(s["xh"], 1)

            def logits(m, conv):
                act.wait_ge(s["lgT"], m + 1)
                if conv is not None:
                    act.wait_ge(s["x3"], conv)
                act.activation(zT, X, ACT.Copy).then_inc(s["lgS"], 1)

            def exps(m):
                act.wait_ge(s["sm"], m + 1)
                act.activation(lg, lg, ACT.Exp).then_inc(s["ex"], 1)

            def weights(m):
                act.wait_ge(s["cx"], m + 1)
                act.activation(combT, X[0:NX], ACT.Copy).then_inc(s["cT"], 1)

            def silu(n, q, c):
                act.wait_ge(s["g"], FC * n + c + 1)
                act.wait_ge(s["al"], FC * n + c)
                act.activation(pr[:], GB(q), ACT.Silu).then_inc(s["silu"], 1)

            def high_act(n, q, c):
                act.wait_ge(s["p"], FC * n + c + 1)
                act.activation(ah[:, q % 2], pr[:], ACT.Copy).then_inc(s["ah"], 1)

            def outputs(e):
                act.wait_ge(s["s2"], FC * (e + 1))
                for m in range(KE):
                    act.activation(backT[:, m], OB(m), ACT.Copy).then_inc(s["oT"], 1)

            def taps_out(r):
                act.wait_ge(s["taps_p"], r + 1)
                act.activation(taps[:, 2 * r:2 * r + 2], X.rearrange("p (m e) -> p m e", e=E), ACT.Copy).then_inc(s["taps_a"], 1)

            split(0)
            act.wait_ge(s["taps_in"], 16)
            act.activation(tw[:, 0:2], tw[:, 0:2], ACT.Sigmoid).then_inc(s["taps_a"], 1)
            for k in range(KE):
                high(0, 0, k)
            split(1)
            logits(0, None)
            exps(0)
            weights(0)
            silu(0, 0, 0)

            def tile(n, parity, epilogue, prologue):
                if epilogue:
                    outputs(n - 1)
                for c in range(1, FC):
                    q = FC * parity + c
                    if first(n) and c + 1 < FC:
                        split(c + 1)
                    high_act(n, q - 1, c - 1)
                    if prologue and c == 20:
                        act.activation(zero[:], zero[:], ACT.Silu)
                    silu(n, q, c)
                    if first(n) and c in (4, 6):
                        taps_out((c - 4) // 2)
                    if epilogue == "conv" and c == 14:
                        act.wait_ge(s["conv_link"], n * CONV_LINKS)
                        act.activation(z[:], z[:], ACT.Silu).then_inc(s["csilu"], 1)
                    if prologue:
                        if c in (13, 15):
                            high(n + 1, 1 - parity, (c - 13) // 2)
                        if c == 17:
                            logits(n + 1, n if epilogue == "conv" else None)
                        if c == 19:
                            exps(n + 1)
                        if c == 24:
                            weights(n + 1)
                high_act(n, FC * parity + FC - 1, FC - 1)
                if prologue:
                    silu(n + 1, FC * parity + FC, 0)

            tiles(act, tile)
            outputs(TT - 1)

        @block.vector
        def _(dve):
            def tap_columns():
                sd, sa, be, ga = (tw[:, i] for i in range(4))
                v = [0]

                def step(ins):
                    v[0] += 1
                    ins.then_inc(s["taps_v"], 1)
                    dve.wait_ge(s["taps_v"], v[0])

                dve.wait_ge(s["taps_a"], 1)
                step(dve.tensor_tensor(sa, sd, sa, ALU.mult))
                step(dve.tensor_tensor(be, be, ga, ALU.mult))
                step(dve.tensor_tensor(be, be, sa, ALU.mult))
                step(dve.tensor_scalar(be, be, float(1.0 / 16) ** 0.5, None, ALU.mult))
                step(dve.tensor_scalar(sa, sa, -1.0, 1.0, ALU.mult, ALU.add))
                for m in range(LAGS):
                    step(dve.reduce_sum(kcol[:, m], be, AX.X))
                    if m < LAGS - 1:
                        step(dve.tensor_tensor(be, be, sa, ALU.mult))

            def tap_diagonals():
                zd = z[:].rearrange("p b e -> p (b e)").rearrange("p (m k n) -> p m k n", m=LAGS, k=KE)
                for m in range(LAGS):
                    for k in range(KE):
                        last = dve.tensor_scalar(zd[:, m, k], ident[:], kcol[:, m, k:k + 1], None, ALU.mult)
                last.then_inc(s["taps_d"], 1)

            def split(c):
                dve.wait_ge(s["wh"], 2 * c + 2)
                dve.tensor_tensor(w1l[:, c].rearrange("p k g f -> p (k g f)"), stage1[:, c % 2, :],
                                  w1h[:, c].bitcast(F32).rearrange("p k g f -> p (k g f)"), ALU.subtract).then_inc(s["wl"], 1)
                dve.tensor_tensor(w2l[:, c], stage2[:, c % 2, :], w2h[:, c].bitcast(F32), ALU.subtract).then_inc(s["wl"], 1)

            def aggregate(which, done):
                for b in range(B):
                    last = dve.bn_aggr(mv[:, which, b], stats[:, which, b])
                last.then_inc(s[done], 1)

            def wait_apart(name, value):
                dve.wait_ge(s[name], value)
                dve.memset(pad[:], 0.0)

            def normalise(which, rows, to, ready, done, m):
                dve.wait_ge(s[ready], m + 1)
                for b in range(B):
                    last = dve.tensor_scalar(to[:, b], rows[:, b], mv[:, which, b, 0:1], rstd[:, which, b:b + 1],
                                             ALU.subtract, ALU.mult)
                last.then_inc(s[done], 1)

            def prologue_stats(m, half):
                if half == 0:
                    dve.wait_ge(s["xp"], 16 * m + 16)
                for b in range(2 * half, 2 * half + 2):
                    last = dve.bn_stats(stats[:, 0, b], xp[:, b])
                if half == 0:
                    return
                last.then_inc(s["plink"], 1)
                wait_apart("plink", m + 1)
                aggregate(0, "pst")

            def low(m, parity, k):
                dve.wait_ge(s["xh"], KE * m + k + 1)
                dve.tensor_tensor(xl[:, parity, k], X, xh[:, parity, k].bitcast(F32), ALU.subtract).then_inc(s["xl"], 1)

            def softmax(m):
                L = X.rearrange("p (b n) -> p b n", n=P)[:, :, 0:NX]
                dve.wait_ge(s["lgX"], m + 1)
                dve.reduce_max(mx[:], L, AX.X).then_inc(s["mx"], 1)
                dve.wait_ge(s["mx"], m + 1)
                dve.tensor_tensor(lg, L, mx[:].unsqueeze(2).to_broadcast([P, B, NX]), ALU.subtract).then_inc(s["sm"], 1)

            def link(m, k, ins, apart=False):
                ins.then_inc(s["link"], 1)
                (wait_apart if apart else lambda a, v: dve.wait_ge(s[a], v))("link", m * ROUTE_LINKS + k)

            pb = prob[:, :, 0:NX]

            def probabilities(m):
                dve.wait_ge(s["ex"], m + 1)
                link(m, 1, dve.reduce_sum(mx[:], lg, AX.X))
                link(m, 2, dve.reciprocal(mx[:], mx[:]))
                link(m, 3, dve.tensor_tensor(pb, lg, mx[:].unsqueeze(2).to_broadcast([P, B, NX]), ALU.mult), True)
                for b in range(B):
                    last = dve.max(top[:, b], prob[:, b, 0:NX])
                link(m, 4, last)
                dve.tensor_copy(top[:, :, TOPK:8], prob[:, :, NX:NX + 2]).then_inc(s["link"], 1)

            def choose(m):
                wait_apart("link", m * ROUTE_LINKS + 5)
                for b in range(B):
                    last = dve.match_replace(rest[:, b], top[:, b], prob[:, b], 0.0)
                link(m, 6, last)
                dve.tensor_tensor(comb, pb, rest[:, :, 0:NX], ALU.subtract).then_inc(s["comb"], 1)

            def product(n, q, c):
                t = pr[:]
                dve.wait_ge(s["silu"], FC * n + c + 1)
                dve.wait_ge(s["u"], FC * n + c + 1)
                if c < FM:
                    dve.tensor_tensor(t, t, UB(q), ALU.mult).then_inc(s["p1"], 1)
                    dve.wait_ge(s["p1"], FM * n + c + 1)
                    dve.wait_ge(s_cb[c % RING], 16 * LOADS[c % RING] * n + 16 * loads_to(c))
                    dve.tensor_tensor(t, t, cbs[:, c % RING], ALU.mult).then_inc(s["p"], 1)
                else:
                    dve.tensor_tensor(t, t, UB(q), ALU.mult).then_inc(s["p"], 1)

            def low_act(n, q, c):
                dve.wait_ge(s["ah"], FC * n + c + 1)
                dve.tensor_tensor(al[:, q % 2], pr[:], ah[:, q % 2].bitcast(F32), ALU.subtract).then_inc(s["al"], 1)

            def residual(e, half):
                if half == 0:
                    dve.wait_ge(s["xe"], 16 * e + 16)
                dve.wait_ge(s["back"], 2 * e + half + 1)
                t = xe[:, 2 * half:2 * half + 2]
                dve.tensor_tensor(t, t, X.rearrange("p (b e) -> p b e", e=E), ALU.add).then_inc(s["x2"], 1)

            for half in range(2):
                prologue_stats(0, half)
            dve.wait_ge(s["gsplit"], 1)
            dve.tensor_tensor(gt_l[:], pr[:, 0:GW], gt_h[:].bitcast(F32), ALU.subtract).then_inc(s["gsplit"], 1)
            normalise(0, xp, xp, "prs", "pxn", 0)
            for k in range(KE):
                low(0, 0, k)
            split(0)
            tap_columns()
            split(1)
            softmax(0)
            probabilities(0)
            choose(0)
            product(0, 0, 0)

            def tile(n, parity, epilogue, prologue):
                for c in range(1, FC):
                    q = FC * parity + c
                    if first(n) and c + 1 < FC:
                        split(c + 1)
                    low_act(n, q - 1, c - 1)
                    product(n, q, c)
                    if first(n) and c == 2:
                        tap_diagonals()
                    if epilogue and c in (4, 6):
                        residual(n - 1, (c - 4) // 2)
                    if epilogue == "conv":
                        if c == 5:
                            dve.wait_ge(s["x2"], 2 * n - 1)
                            for b in range(2):
                                dve.bn_stats(stats[:, 1, b], xe[:, b])
                        if c == 7:
                            dve.wait_ge(s["x2"], 2 * n)
                            for b in range(2, B):
                                last = dve.bn_stats(stats[:, 1, b], xe[:, b])
                            last.then_inc(s["clink"], 1)
                            wait_apart("clink", n)
                            aggregate(1, "cst")
                        if c == 8:
                            normalise(1, xe, backY, "crs", "cy", n - 1)
                        if c == 16:
                            dve.wait_ge(s["csilu"], n)
                            dve.tensor_tensor(xe[:], xe[:], z[:], ALU.add).then_inc(s["x3"], 1)
                    if prologue:
                        if c in (9, 10):
                            prologue_stats(n + 1, c - 9)
                        if c == 11:
                            normalise(0, xp, xp, "prs", "pxn", n + 1)
                        if c in (13, 15):
                            low(n + 1, 1 - parity, (c - 13) // 2)
                        if c == 19:
                            softmax(n + 1)
                        if c == 21:
                            probabilities(n + 1)
                        if c == 22:
                            choose(n + 1)
                low_act(n, FC * parity + FC - 1, FC - 1)
                if prologue:
                    product(n + 1, FC * parity + FC, 0)

            tiles(dve, tile)
            for half in range(2):
                residual(TT - 1, half)

        @block.tensor
        def _(pe):
            def taps_to_all(r):
                pe.wait_ge(s["taps_d"], 1)
                if r:
                    pe.wait_ge(s["taps_a"], 2)
                zd = z[:].rearrange("p b e -> p (b e)")
                for j in range(2 * KE):
                    at_ = (2 * KE * r + j) * P
                    last = pe.matmul(X[:, j * P:(j + 1) * P], tmp[:, 0:P], zd[:, at_:at_ + P], start=True, stop=True)
                last.then_inc(s["taps_p"], 1)

            pe.wait_ge(s["made"], 6)
            pe.wait_ge(s["gsplit"], 2)

            def three(out, lhs, rhs, done):
                n = 0
                for a, b in ((0, 0), (0, 1), (1, 0)):
                    for k in range(KE):
                        last = pe.matmul(out, lhs(a, k), rhs(b, k), start=n == 0, stop=n == 3 * KE - 1)
                        n += 1
                last.then_inc(s[done], 1)

            x_of = lambda parity: lambda b, k: (xh, xl)[b][:, parity, k]

            def gate_up(n, parity, q, c):
                for g, out, done in ((0, GB(q), "g"), (1, UB(q), "u")):
                    three(out, lambda a, k: (w1h, w1l)[a][:, c, k, g], x_of(parity), done)

            def down(n, q, c):
                pe.wait_ge(s["al"], FC * n + c + 1)
                if c == 0:
                    pe.wait_ge(s["oT"], KE * n)
                for m in range(KE):
                    for j, (w, t) in enumerate(((w2h, ah), (w2h, al), (w2l, ah))):
                        last = pe.matmul(OB(m), w[:, c, m * P:(m + 1) * P], t[:, q % 2], start=c == 0 and j == 0,
                                         stop=c == FC - 1 and j == 2)
                last.then_inc(s["s2"], 1)

            def transpose_rows(m, k):
                if k == 0:
                    pe.wait_ge(s["pxn"], m + 1)
                else:
                    pe.wait_ge(s["xl"], KE * m + 1)
                for b in range(B):
                    last = pe.transpose(X[:, b * P:(b + 1) * P], xp[:, b, k * P:(k + 1) * P], ident[:])
                last.then_inc(s["tx"], 1)

            def gate_logits(m, parity):
                pe.wait_ge(s["xl"], KE * m + KE)
                three(X, lambda a, k: (gt_h, gt_l)[a][:, k * NX:k * NX + P], x_of(parity), "lgT")

            def transpose_logits(m):
                pe.wait_ge(s["lgS"], m + 1)
                for b in range(B):
                    last = pe.transpose(X[:, b * P:(b + 1) * P], zT[:, b * P:(b + 1) * P], ident[:])
                last.then_inc(s["lgX"], 1)

            def transpose_weights(m):
                pe.wait_ge(s["comb"], m + 1)
                for b in range(B):
                    last = pe.transpose(X[0:NX, b * P:(b + 1) * P], prob[:, b, 0:NX], ident[:])
                last.then_inc(s["cx"], 1)

            def transpose_back(e, half):
                if half == 0:
                    pe.wait_ge(s["oT"], KE * (e + 1))
                else:
                    pe.wait_ge(s["x2"], 2 * e + 1)
                for j in range(2):
                    b = 2 * half + j
                    for m in range(KE):
                        last = pe.transpose(X[:, j * E + m * P:j * E + (m + 1) * P], backT[:, m, b * P:(b + 1) * P], ident[:])
                last.then_inc(s["back"], 1)

            for k in range(KE):
                transpose_rows(0, k)
            gate_logits(0, 0)
            transpose_logits(0)
            pe.wait_ge(s["wl"], 2)
            gate_up(0, 0, 0, 0)
            transpose_weights(0)

            def tile(n, parity, epilogue, prologue):
                for c in range(1, FC):
                    q = FC * parity + c
                    if first(n):
                        pe.wait_ge(s["wl"], 2 * c + 2)
                    gate_up(n, parity, q, c)
                    down(n, q - 1, c - 1)
                    if first(n) and c in (4, 6):
                        taps_to_all((c - 4) // 2)
                    if first(n) and c == 8:
                        pe.wait_ge(s["taps_a"], 3)
                    if epilogue and c in (3, 5):
                        transpose_back(n - 1, (c - 3) // 2)
                    if prologue:
                        if c in (12, 14):
                            transpose_rows(n + 1, (c - 12) // 2)
                        if c == 16:
                            gate_logits(n + 1, 1 - parity)
                        if c == 18:
                            transpose_logits(n + 1)
                        if c == 23:
                            transpose_weights(n + 1)
                if prologue:
                    gate_up(n + 1, 1 - parity, FC * parity + FC, 0)
                down(n, FC * parity + FC - 1, FC - 1)

            tiles(pe, tile)
            for half in range(2):
                transpose_back(TT - 1, half)


CONV_LINKS = 2 * sum(B - m for m in range(1, LAGS)) + B
ROUTE_LINKS = 6


def rope_table():
    inv = (1.0 / np.float32(10000.0) ** (np.arange(0, D, 2, dtype=np.float32) / np.float32(D))).astype(np.float32)
    t = np.arange(N, dtype=np.float32)[:, None] * inv[None, :]
    c, s = np.cos(t), np.sin(t)
    both = np.stack([np.concatenate([c, c], 1), np.concatenate([-s, s], 1)])
    return np.ascontiguousarray(both.reshape(2, NT, P, D).transpose(2, 0, 1, 3)).astype(np.float32)


def kernel(L0_attn_a_x, L0_attn_a_w_qkv, L0_attn_a_w_out, L0_attn_a_ln_scale, L0_attn_a_ln_bias,
           L0_attn_b_delta, L0_attn_b_alpha, L0_attn_b_beta, L0_attn_b_gamma, L0_ffn_gate_w,
           L0_ffn_w1, L0_ffn_w2, L0_ffn_shared_w1, L0_ffn_shared_w2):
    import concourse.bacc as bacc
    from concourse.bass_utils import run_bass_kernel_spmd

    def blocks(w):
        return w.reshape(-1, P, w.shape[-1]).transpose(1, 0, 2)

    pad = FC * P - FM * P - SH
    w1 = np.asarray(L0_ffn_w1).reshape(NX, 2, IH, E)
    sw1 = np.asarray(L0_ffn_shared_w1).reshape(2, SH, E)
    both = [np.concatenate([w1[:, g].reshape(NX * IH, E), sw1[g], np.zeros((pad, E), np.float32)]) for g in range(2)]
    w1s = np.stack(both).reshape(2, FC, P, KE, P).transpose(4, 1, 3, 0, 2).reshape(P, FC, KE * 2 * P)
    w2s = np.concatenate([np.asarray(L0_ffn_w2).transpose(0, 2, 1).reshape(NX * IH, E),
                          np.asarray(L0_ffn_shared_w2).T, np.zeros((pad, E), np.float32)])
    gate = np.concatenate([*np.asarray(L0_ffn_gate_w).T.reshape(KE, P, NX), np.zeros((P, P - NX), np.float32)], 1)
    taps = np.stack([np.asarray(a).reshape(KE, P, 16) for a in
                     (L0_attn_b_delta, L0_attn_b_alpha, L0_attn_b_beta, L0_attn_b_gamma)])
    arrays = {
        "x": np.asarray(L0_attn_a_x).reshape(B, NT, P, E),
        "w_qkv": blocks(np.asarray(L0_attn_a_w_qkv)),
        "w_out": blocks(np.asarray(L0_attn_a_w_out)),
        "ln_affine": np.stack([np.asarray(L0_attn_a_ln_scale), np.asarray(L0_attn_a_ln_bias)]),
        "rope": rope_table(),
        "ident": np.eye(P, dtype=np.float32),
        "w1": w1s,
        "w2": blocks(w2s),
        "gate": gate,
        "taps": taps.transpose(2, 0, 1, 3).reshape(P, 4 * KE * 16),
    }
    arrays = {n: np.ascontiguousarray(a) for n, a in arrays.items()}
    nc = bacc.Bacc("TRN2", target_bir_lowering=False, num_devices=1)
    t = {n: nc.dram_tensor(n, a.shape, mybir.dt.from_np(a.dtype), kind="ExternalInput").ap() for n, a in arrays.items()}
    x1 = nc.dram_tensor("x1", (B, NT, P, E), F32, kind="Internal").ap()
    weights_t = nc.dram_tensor("weights_t", (NX, B * P), F32, kind="Internal").ap()
    x3 = nc.dram_tensor("x3", (B, NT, P, E), F32, kind="Internal").ap()
    out = nc.dram_tensor("out", (B, NT, P, E), F32, kind="ExternalOutput").ap()
    attention(nc, t["x"], t["w_qkv"], t["w_out"], t["ln_affine"], t["rope"], t["ident"], x1)
    feed_forward(nc, x1, t["w1"], t["w2"], t["gate"], t["taps"], t["ident"], weights_t, x3, out)
    r = run_bass_kernel_spmd(nc, [arrays], core_ids=[0])
    return r.results[0]["out"].reshape(B, N, E)
```
